# Optimizing a Trainium2 kernel written in Bass

```python
import numpy as np
import jax
import jax.numpy as jnp

def _softmax(x, axis=-1):
    return jax.nn.softmax(x, axis=axis)

def _gelu(x):
    return jax.nn.gelu(x, approximate=True)

def _silu(x):
    return jax.nn.silu(x)

def _sigmoid(x):
    return jax.nn.sigmoid(x)

def _layernorm(x, axis=-1, eps=1e-05):
    m = jnp.mean(x, axis=axis, keepdims=True)
    v = jnp.var(x, axis=axis, keepdims=True)
    return (x - m) / jnp.sqrt(v + eps)

def _scatter_add(tgt, idx, src, axis=0):
    return tgt.at[idx].add(src)

def _segment_sum(src, seg, n):
    return jax.ops.segment_sum(src, seg, n)
kernel_name = 'mk_seq_preln_d1_jaxref_r8_9670b2'

def setup_inputs(seed: int=0):
    np.random.seed(seed)
    _w = jnp.asarray

    def _L0_attn_setup():
        import jax, jax.numpy as jnp
        import numpy as np
        from math import sqrt
        EMBED_DIM = 128
        NUM_HEADS = 16
        HEAD_DIM = EMBED_DIM // NUM_HEADS
        CAUSAL = True
        key = jax.random.key(seed)
        ks = jax.random.split(key, 5)
        B, S, E = (2, 256, EMBED_DIM)
        x = jax.random.normal(ks[0], (B, S, E), dtype=jnp.float32)
        scale = 1.0 / sqrt(E)
        Wq = jax.random.normal(ks[1], (E, E), dtype=jnp.float32) * scale
        Wk = jax.random.normal(ks[2], (E, E), dtype=jnp.float32) * scale
        Wv = jax.random.normal(ks[3], (E, E), dtype=jnp.float32) * scale
        Wo = jax.random.normal(ks[4], (E, E), dtype=jnp.float32) * scale
        return {'x': x, 'Wq': Wq, 'Wk': Wk, 'Wv': Wv, 'Wo': Wo}
    _L0_attn_in = _L0_attn_setup()

    def _L0_ffn_setup():
        import jax, jax.numpy as jnp
        import numpy as np
        DIM = 128
        DEPTH = 6
        HEADS = 16
        DIM_HEAD = 64
        WINDOW = 32
        INNER = HEADS * DIM_HEAD
        DIM_INNER = int(DIM * 4 * 2 / 3)
        QK_SCALE = 8.0

        def shift_tokens(t):
            a, s = jnp.split(t, 2, -1)
            s = jnp.pad(s, ((0, 0), (1, 0), (0, 0)))[:, :-1]
            return jnp.concatenate([a, s], -1)

        def l2norm(t):
            return t / jnp.maximum(jnp.linalg.norm(t, axis=-1, keepdims=True), 1e-12)

        def rotate_half(x):
            x1, x2 = jnp.split(x, 2, -1)
            return jnp.concatenate([-x2, x1], -1)

        def rotary_tables(n):
            half = jnp.arange(0, DIM_HEAD, 2, dtype=jnp.float32)
            inv_freq = 1.0 / 10000.0 ** (half / DIM_HEAD)
            t = jnp.arange(n, dtype=jnp.float32)
            freqs = t[:, None] * inv_freq[None, :]
            freqs = jnp.concatenate([freqs, freqs], -1)
            base_scale = (half + 0.4 * DIM_HEAD) / (1.4 * DIM_HEAD)
            power = (t - n // 2) / (WINDOW // 2)
            scale = base_scale[None, :] ** power[:, None]
            scale = jnp.concatenate([scale, scale], -1)
            return (freqs, scale)

        def local_attention(q, k, v):
            b, h, n, d = q.shape
            w = WINDOW
            nw = n // w
            bq = q.reshape(b, h, nw, w, d)
            bk = k.reshape(b, h, nw, w, d)
            bv = v.reshape(b, h, nw, w, d)

            def look(t):
                p = jnp.pad(t, ((0, 0), (0, 0), (1, 0), (0, 0), (0, 0)))
                return jnp.concatenate([p[:, :, :nw], p[:, :, 1:]], axis=3)
            bk2, bv2 = (look(bk), look(bv))
            seq = jnp.arange(n).reshape(nw, w)
            seq_p = jnp.pad(seq, ((1, 0), (0, 0)), constant_values=-1)
            jt = jnp.concatenate([seq_p[:nw], seq_p[1:]], axis=1)
            it = seq[:, :, None]
            jb = jt[:, None, :]
            mask = (it < jb) | (it > jb + w) | (jb == -1)
            sim = jnp.einsum('bhwie,bhwje->bhwij', bq, bk2) * QK_SCALE
            sim = jnp.where(mask, -jnp.finfo(sim.dtype).max, sim)
            attn = jax.nn.softmax(sim, -1)
            out = jnp.einsum('bhwij,bhwje->bhwie', attn, bv2)
            return out.reshape(b, h, n, d)

        def attn_layer(x, Wqkv, qs, ksc, Wo):
            b, n, _ = x.shape
            qkv = x @ Wqkv
            q, k, v = jnp.split(qkv, 3, -1)
            sh = lambda t: t.reshape(b, n, HEADS, DIM_HEAD).transpose(0, 2, 1, 3)
            q, k, v = (sh(q), sh(k), sh(v))
            q = l2norm(q) * qs
            k = l2norm(k) * ksc
            freqs, scale = rotary_tables(n)
            cos, sin = (jnp.cos(freqs), jnp.sin(freqs))
            q = q * cos * scale + rotate_half(q) * sin * scale
            inv = 1.0 / scale
            k = k * cos * inv + rotate_half(k) * sin * inv
            out = local_attention(q, k, v)
            out = out.transpose(0, 2, 1, 3).reshape(b, n, INNER)
            return out @ Wo

        def ffn_layer(x, g, bln, W1, b1, W2, b2):
            mu = x.mean(-1, keepdims=True)
            var = ((x - mu) ** 2).mean(-1, keepdims=True)
            xn = (x - mu) / jnp.sqrt(var + 1e-05) * g + bln
            hg = xn @ W1 + b1
            a, gate = jnp.split(hg, 2, -1)
            return a * jax.nn.gelu(gate, approximate=False) @ W2 + b2
        key = jax.random.key(seed)
        ks = jax.random.split(key, 8)
        B, N = (2, 256)
        init = lambda k, shape: jax.random.normal(k, shape, jnp.float32) * 0.02
        return {'x': jax.random.normal(ks[0], (B, N, DIM), jnp.float32), 'Wqkv': init(ks[1], (DEPTH, DIM, 3 * INNER)), 'q_scale': jnp.ones((DEPTH, DIM_HEAD), jnp.float32), 'k_scale': jnp.ones((DEPTH, DIM_HEAD), jnp.float32), 'Wo': init(ks[2], (DEPTH, INNER, DIM)), 'ln_g': jnp.ones((DEPTH, DIM), jnp.float32), 'ln_b': jnp.zeros((DEPTH, DIM), jnp.float32), 'W1': init(ks[3], (DEPTH, DIM, 2 * DIM_INNER)), 'b1': jnp.zeros((DEPTH, 2 * DIM_INNER), jnp.float32), 'W2': init(ks[4], (DEPTH, DIM_INNER, DIM)), 'b2': jnp.zeros((DEPTH, DIM), jnp.float32)}
    _L0_ffn_in = _L0_ffn_setup()
    _d = {'L0_attn_x': _L0_attn_in['x'], 'L0_attn_Wq': _L0_attn_in['Wq'], 'L0_attn_Wk': _L0_attn_in['Wk'], 'L0_attn_Wv': _L0_attn_in['Wv'], 'L0_attn_Wo': _L0_attn_in['Wo'], 'L0_ffn_Wqkv': _L0_ffn_in['Wqkv'], 'L0_ffn_q_scale': _L0_ffn_in['q_scale'], 'L0_ffn_k_scale': _L0_ffn_in['k_scale'], 'L0_ffn_Wo': _L0_ffn_in['Wo'], 'L0_ffn_ln_g': _L0_ffn_in['ln_g'], 'L0_ffn_ln_b': _L0_ffn_in['ln_b'], 'L0_ffn_W1': _L0_ffn_in['W1'], 'L0_ffn_b1': _L0_ffn_in['b1'], 'L0_ffn_W2': _L0_ffn_in['W2'], 'L0_ffn_b2': _L0_ffn_in['b2']}
    _x0 = _d['L0_attn_x']
    _d['L0_attn_x'] = jax.random.normal(jax.random.fold_in(jax.random.key(seed), 1), (16, 256, 128), dtype=_x0.dtype)
    del _x0
    return _d

def reference(L0_attn_x, L0_attn_Wq, L0_attn_Wk, L0_attn_Wv, L0_attn_Wo, L0_ffn_Wqkv, L0_ffn_q_scale, L0_ffn_k_scale, L0_ffn_Wo, L0_ffn_ln_g, L0_ffn_ln_b, L0_ffn_W1, L0_ffn_b1, L0_ffn_W2, L0_ffn_b2):

    def _L0_attn_ref(x, Wq, Wk, Wv, Wo):
        import jax, jax.numpy as jnp
        import numpy as np
        from math import sqrt
        EMBED_DIM = 128
        NUM_HEADS = 16
        HEAD_DIM = EMBED_DIM // NUM_HEADS
        CAUSAL = True
        B, S, E = x.shape
        H, D = (NUM_HEADS, HEAD_DIM)

        def proj(W):
            y = jnp.einsum('bse,fe->bsf', x, W)
            return y.reshape(B, S, H, D).transpose(0, 2, 1, 3)
        q, k, v = (proj(Wq), proj(Wk), proj(Wv))
        scores = jnp.einsum('bhsd,bhtd->bhst', q, k)
        if CAUSAL:
            mask = jnp.triu(jnp.ones((S, S), dtype=bool), k=1)
            scores = jnp.where(mask, -jnp.inf, scores)
        attn = jax.nn.softmax(scores / sqrt(D), axis=-1)
        out = jnp.einsum('bhst,bhtd->bhsd', attn, v)
        out = out.transpose(0, 2, 1, 3).reshape(B, S, E)
        return jnp.einsum('bse,fe->bsf', out, Wo)

    def _L0_ffn_ref(x, Wqkv, q_scale, k_scale, Wo, ln_g, ln_b, W1, b1, W2, b2):
        import jax, jax.numpy as jnp
        import numpy as np
        DIM = 128
        DEPTH = 6
        HEADS = 16
        DIM_HEAD = 64
        WINDOW = 32
        INNER = HEADS * DIM_HEAD
        DIM_INNER = int(DIM * 4 * 2 / 3)
        QK_SCALE = 8.0

        def shift_tokens(t):
            a, s = jnp.split(t, 2, -1)
            s = jnp.pad(s, ((0, 0), (1, 0), (0, 0)))[:, :-1]
            return jnp.concatenate([a, s], -1)

        def l2norm(t):
            return t / jnp.maximum(jnp.linalg.norm(t, axis=-1, keepdims=True), 1e-12)

        def rotate_half(x):
            x1, x2 = jnp.split(x, 2, -1)
            return jnp.concatenate([-x2, x1], -1)

        def rotary_tables(n):
            half = jnp.arange(0, DIM_HEAD, 2, dtype=jnp.float32)
            inv_freq = 1.0 / 10000.0 ** (half / DIM_HEAD)
            t = jnp.arange(n, dtype=jnp.float32)
            freqs = t[:, None] * inv_freq[None, :]
            freqs = jnp.concatenate([freqs, freqs], -1)
            base_scale = (half + 0.4 * DIM_HEAD) / (1.4 * DIM_HEAD)
            power = (t - n // 2) / (WINDOW // 2)
            scale = base_scale[None, :] ** power[:, None]
            scale = jnp.concatenate([scale, scale], -1)
            return (freqs, scale)

        def local_attention(q, k, v):
            b, h, n, d = q.shape
            w = WINDOW
            nw = n // w
            bq = q.reshape(b, h, nw, w, d)
            bk = k.reshape(b, h, nw, w, d)
            bv = v.reshape(b, h, nw, w, d)

            def look(t):
                p = jnp.pad(t, ((0, 0), (0, 0), (1, 0), (0, 0), (0, 0)))
                return jnp.concatenate([p[:, :, :nw], p[:, :, 1:]], axis=3)
            bk2, bv2 = (look(bk), look(bv))
            seq = jnp.arange(n).reshape(nw, w)
            seq_p = jnp.pad(seq, ((1, 0), (0, 0)), constant_values=-1)
            jt = jnp.concatenate([seq_p[:nw], seq_p[1:]], axis=1)
            it = seq[:, :, None]
            jb = jt[:, None, :]
            mask = (it < jb) | (it > jb + w) | (jb == -1)
            sim = jnp.einsum('bhwie,bhwje->bhwij', bq, bk2) * QK_SCALE
            sim = jnp.where(mask, -jnp.finfo(sim.dtype).max, sim)
            attn = jax.nn.softmax(sim, -1)
            out = jnp.einsum('bhwij,bhwje->bhwie', attn, bv2)
            return out.reshape(b, h, n, d)

        def attn_layer(x, Wqkv, qs, ksc, Wo):
            b, n, _ = x.shape
            qkv = x @ Wqkv
            q, k, v = jnp.split(qkv, 3, -1)
            sh = lambda t: t.reshape(b, n, HEADS, DIM_HEAD).transpose(0, 2, 1, 3)
            q, k, v = (sh(q), sh(k), sh(v))
            q = l2norm(q) * qs
            k = l2norm(k) * ksc
            freqs, scale = rotary_tables(n)
            cos, sin = (jnp.cos(freqs), jnp.sin(freqs))
            q = q * cos * scale + rotate_half(q) * sin * scale
            inv = 1.0 / scale
            k = k * cos * inv + rotate_half(k) * sin * inv
            out = local_attention(q, k, v)
            out = out.transpose(0, 2, 1, 3).reshape(b, n, INNER)
            return out @ Wo

        def ffn_layer(x, g, bln, W1, b1, W2, b2):
            mu = x.mean(-1, keepdims=True)
            var = ((x - mu) ** 2).mean(-1, keepdims=True)
            xn = (x - mu) / jnp.sqrt(var + 1e-05) * g + bln
            hg = xn @ W1 + b1
            a, gate = jnp.split(hg, 2, -1)
            return a * jax.nn.gelu(gate, approximate=False) @ W2 + b2
        for i in range(DEPTH):
            x = attn_layer(shift_tokens(x), Wqkv[i], q_scale[i], k_scale[i], Wo[i]) + x
            x = ffn_layer(shift_tokens(x), ln_g[i], ln_b[i], W1[i], b1[i], W2[i], b2[i]) + x
        return x
    x = L0_attn_x
    x = x + _L0_attn_ref(_layernorm(x, axis=-1), L0_attn_Wq, L0_attn_Wk, L0_attn_Wv, L0_attn_Wo)
    x = x + _L0_ffn_ref(_layernorm(x, axis=-1), L0_ffn_Wqkv, L0_ffn_q_scale, L0_ffn_k_scale, L0_ffn_Wo, L0_ffn_ln_g, L0_ffn_ln_b, L0_ffn_W1, L0_ffn_b1, L0_ffn_W2, L0_ffn_b2)
    return x

_drawn_inputs = setup_inputs


def setup_inputs(seed=0):
    import zlib

    import numpy as np

    out = dict(_drawn_inputs(seed))
    spreads = {'L0_ffn_q_scale': (1.0, 0.6),
     'L0_ffn_k_scale': (1.0, 0.6),
     'L0_ffn_ln_g': (1.0, 0.6),
     'L0_ffn_ln_b': (0.0, 0.8),
     'L0_ffn_b1': (0.0, 0.8),
     'L0_ffn_b2': (0.0, 0.1)}
    factors = {'L0_ffn_W1': 3.694, 'L0_ffn_W2': 3.626}
    for name, (base, spread) in spreads.items():
        noise = np.random.default_rng([zlib.crc32(name.encode()), seed]).standard_normal(out[name].shape)
        drawn = base * np.exp(spread * noise) if base else spread * noise
        out[name] = jnp.asarray(drawn.astype(out[name].dtype))
    for name, factor in factors.items():
        out[name] = (out[name] * factor).astype(out[name].dtype)
    return out
```

```python
from contextlib import ExitStack

import concourse.bass as bass
from concourse import mybir

F32 = mybir.dt.float32
BF16 = mybir.dt.bfloat16
ALU = mybir.AluOpType
ACT = mybir.ActivationFunctionType
AX = mybir.AxisListType
P = 128

SEQS, SEQ, DIM = 16, 256, 128
TILES = SEQ // P
HA, DA = 16, 8
DEPTH, HEADS, DH = 6, 16, 64
INNER = HEADS * DH
PAIRS = HEADS // 2
WIN = 32
NWIN = P // WIN
FF = int(DIM * 4 * 2 / 3)
FCH = [(c, min(P, FF - c)) for c in range(0, FF, P)]
NF = len(FCH)
QK_SCALE = 8.0
A_SCALE = 1.0 / float(DA) ** 0.5
EPS = 1e-5
NORM_FLOOR = 1e-12
TABLE_SET = "natural_log_exp_and_others"


def need(eng, sem, value):
    if isinstance(value, int) and value <= 0:
        return
    eng.wait_ge(sem, value)


def need_apart(eng, idle, sem, value):
    need(eng, sem, value)
    eng.sem_inc(idle, 1)


def build(nc, x_in, wq_t, wk_t, wv_t, wo_t, wqkv, q_scale, k_scale, wo2, ln_g, ln_b, w1, b1, w2, b2,
          c_ident, c_winmask, c_causal, c_headmask, c_rot, out):
    with ExitStack() as ctx:
        def sb(name, shape, dt=F32):
            return ctx.enter_context(nc.sbuf_tensor(name, shape, dt))

        def sem(name):
            return ctx.enter_context(nc.semaphore(name))

        ps = ctx.enter_context(nc.psum_tensor("ps", [P, 8, 512], F32))

        xres = sb("xres", [P, SEQS * TILES, DIM])
        x1 = sb("x1", [P, SEQS * TILES, DIM])
        ident = sb("ident", [P, P])
        ident_h = sb("ident_h", [P, P], BF16)
        wmask_f = sb("wmask_f", [P, 2, 2 * WIN])
        wmask = sb("wmask", [P, 2, 2 * WIN], BF16)
        causal_f = sb("causal_f", [P, 2 * P])
        causal = sb("causal", [P, 2 * P], BF16)
        headmask = sb("headmask", [P, HA])
        rot = sb("rot", [P, TILES, 4, DH])
        Wqkv = sb("Wqkv", [P, 3 * INNER])
        Wo = sb("Wo", [P, PAIRS, DIM])
        W1 = sb("W1", [P, 2 * FF])
        W2 = sb("W2", [P, NF, DIM])
        lng = sb("lng", [P, 1])
        lnb = sb("lnb", [P, 1])
        b1s = sb("b1s", [P, 2, NF])
        qks = sb("qks", [P, 2, DH])
        tab = sb("tab", [P, TILES, 4, DH])
        area1 = sb("area1", [P, 3, 2048])
        SQ, QH = area1[:, 0, :], area1[:, 1, :]
        AQ = [area1[:, 2, :], sb("AQb", [P, 2048])[:, :]]
        E0 = area1[:, 0, :].rearrange("p (h k) -> p h k", h=HA)
        E1 = area1[:, 1:3, :].rearrange("p a k -> p (a k)").rearrange("p (h k) -> p h k", h=HA)
        area2 = sb("area2", [P, 4096])
        BQ = area2[:, 0:2048]
        V = area2[:, 2048:4096].rearrange("p (t n) -> p t n", t=TILES)
        PT0 = area2[:, :].rearrange("p (h q) -> p h q", h=HA)
        area3 = sb("area3", [P, 4096])
        Pr = area3[:, 0:2048].rearrange("p (t n) -> p t n", t=TILES)
        oT = area3[:, 2048:4096].rearrange("p (t c n) -> p t c n", t=TILES, c=PAIRS)
        KM = area3[:, :].rearrange("p (h k) -> p h k", h=HA)
        area4 = sb("area4", [P, 2048])
        PT1 = area4[:, :].rearrange("p (h q) -> p h q", h=HA)
        qT = area4[:, 0:1024].rearrange("p (c n) -> p c n", c=PAIRS)
        PTr = area4[:, 1024:2048].rearrange("p (h b i) -> p h b i", h=HEADS, b=2)
        kbd = sb("kbd", [P, PAIRS, 2, WIN + SEQ])
        BD = sb("BD", [P, TILES, HEADS, P])
        BB = sb("BB", [P, HEADS, WIN])
        xst = sb("xst", [P, TILES, DIM])
        xsT = sb("xsT", [P, SEQ + 1])
        x2s = sb("x2s", [P, TILES, DIM])
        x2T = sb("x2T", [P, SEQ + 1])
        xn = sb("xn", [P, TILES, DIM])
        xnT = sb("xnT", [P, SEQ])
        G = sb("G", [P, NF, SEQ])
        H = sb("H", [P, NF, SEQ])
        ss = sb("ss", [P, 5, 2 * HEADS])
        inv = sb("inv", [P, 2 * HEADS])
        mx = sb("mx", [P, HEADS])
        lsum = sb("lsum", [P, 2, HEADS])
        stats = sb("stats", [P, TILES, 6])
        mv = sb("mv", [P, TILES, 2])
        lw = sb("lw", [P, 6, TILES])
        xh = sb("xh", [P, TILES, DIM])
        xhT = sb("xhT", [P, SEQ])
        AqT = sb("AqT", [P, SEQ])
        AkT = sb("AkT", [P, SEQ])
        Vp = sb("Vp", [P, TILES, HA, 32])
        AoT = sb("AoT", [P, 4 * SEQ])
        Arl = sb("Arl", [P, 32])
        AoN = sb("AoN", [P, 4, SEQ])
        Wa = sb("Wa", [P, 3, DIM])
        Wap = sb("Wap", [P, 4, DIM])
        nmx = sb("nmx", [P, 2, 2, HA])

        names = ("d_x d_wa d_c d_qkv d_qks d_wo d_ln d_ff d_out i_const i_zero i_pad i_dve i_pool "
                 "a_lnc a_lnr a_lnn a_xh a_xt a_xe a_qk a_qe a_ke a_km a_v a_ve a_s a_mx a_nm a_e a_t a_te "
                 "a_pv a_oe a_rc a_mu a_on a_wo a_x1 b_lnc b_lnr b_lnn "
                 "s_x s_st s_xt s_xe s_pq s_pk s_pv s_sqq s_sqk s_rq s_rk s_fl s_lg s_iv s_nw s_inv s_qh s_kh "
                 "s_aq s_ak s_bq s_bk s_rot s_tr s_te s_qe s_ke s_sc s_mx s_sub s_exp s_sum s_rl s_pn s_T s_bdc s_bdp "
                 "s_o s_oe s_ve s_wo s_r1 s_x2 s_x2e s_bk2 s_lnc s_lnr s_lnn s_ln s_xn s_xne s_h s_gl s_g s_y s_xc "
                 "s_tab s_fin s_exa")
        S = {n: sem(n) for n in names.split()}
        (d_x, d_wa, d_c, d_qkv, d_qks, d_wo, d_ln, d_ff, d_out, i_const, i_zero, i_pad, i_dve, i_pool,
         a_lnc, a_lnr, a_lnn, a_xh, a_xt, a_xe, a_qk, a_qe, a_ke, a_km, a_v, a_ve, a_s, a_mx, a_nm, a_e, a_t, a_te,
         a_pv, a_oe, a_rc, a_mu, a_on, a_wo, a_x1, b_lnc, b_lnr, b_lnn,
         s_x, s_st, s_xt, s_xe, s_pq, s_pk, s_pv, s_sqq, s_sqk, s_rq, s_rk, s_fl, s_lg, s_iv, s_nw, s_inv, s_qh, s_kh,
         s_aq, s_ak, s_bq, s_bk, s_rot, s_tr, s_te, s_qe, s_ke, s_sc, s_mx, s_sub, s_exp, s_sum, s_rl, s_pn, s_T,
         s_bdc, s_bdp, s_o, s_oe, s_ve, s_wo, s_r1, s_x2, s_x2e, s_bk2, s_lnc, s_lnr, s_lnn, s_ln, s_xn, s_xne,
         s_h, s_gl, s_g, s_y, s_xc, s_tab, s_fin, s_exa) = [S[n] for n in names.split()]

        PJ = [ps[:, 0:2, :].rearrange("p a b -> p (a b)"), ps[:, 2:4, :].rearrange("p a b -> p (a b)")]
        SC = ps[:, 4:6, :]
        TR = [ps[:, 6, :], ps[:, 7, :]]

        N_CONST = 5
        N_WA = 7
        N_FF = 8
        block = ctx.enter_context(nc.Block())

        def stack_steps(eng, step):
            step(0, 0, True, False, False, 0)
            step(1, 1, True, True, False, 0)

            def layer_body(base, layer):
                with eng.Fori(0, SEQS - 2) as u:
                    n = eng.snap(base + u + 2)
                    step(n, u + 2, True, True, True, layer)
            with eng.Fori(0, DEPTH - 1) as L:
                layer_body(L * SEQS, L)
                step(eng.snap(L * SEQS + SEQS), 0, True, True, True, L)
                step(eng.snap(L * SEQS + SEQS + 1), 1, True, True, True, L)
            layer_body((DEPTH - 1) * SEQS, DEPTH - 1)
            step(DEPTH * SEQS, 0, False, True, True, DEPTH - 1)
            step(DEPTH * SEQS + 1, 1, False, False, True, DEPTH - 1)

        def unit(u, back):
            if isinstance(u, int):
                k = (u - back) % SEQS * TILES
                return slice(k, k + TILES)
            return bass.ds((u - back) * TILES, TILES)

        @block.sync
        def _(sp):
            sp.dma_start(xres[:, :, :], x_in.rearrange("b (t p) e -> p (b t) e", p=P)).then_inc(d_x, 16)
            for i, w in enumerate((wq_t, wk_t, wv_t)):
                sp.dma_start(Wa[:, i, :], w).then_inc(d_wa, 16)
            for src, dst in ((c_ident, ident[:, :]), (c_causal, causal_f[:, :]),
                             (c_winmask, wmask_f[:, :, :]), (c_headmask, headmask[:, :]),
                             (c_rot, rot[:, :, :, :])):
                sp.dma_start(dst, src).then_inc(d_c, 16)
            sp.wait_ge(i_pad, 2)
            wo_rows = wo_t.rearrange("(c g d) n -> g d c n", g=4, d=DA)
            for g in range(4):
                sp.dma_start(Wap[32 * g:32 * g + DA, :, :], wo_rows[g]).then_inc(d_wa, 16)

            def load_qkv(l):
                sp.dma_start(Wqkv[:, :], wqkv[l]).then_inc(d_qkv, 16)

            def load_scales(l):
                sp.dma_start(qks[:, 0, :], q_scale[l].partition_broadcast(P)).then_inc(d_qks, 16)
                sp.dma_start(qks[:, 1, :], k_scale[l].partition_broadcast(P)).then_inc(d_qks, 16)

            def load_wo(l):
                sp.dma_start(Wo[:, :, :], wo2[l].rearrange("(c p) n -> p c n", p=P)).then_inc(d_wo, 16)

            def load_ln(l):
                sp.dma_start(lng[:, :], ln_g[l].unsqueeze(1)).then_inc(d_ln, 16)
                sp.dma_start(lnb[:, :], ln_b[l].unsqueeze(1)).then_inc(d_ln, 16)

            def load_ff(l):
                sp.dma_start(W1[:, :], w1[l]).then_inc(d_ff, 16)
                last = FCH[-1]
                sp.dma_start(W2[:, 0:NF - 1, :], w2[l][0:last[0], :].rearrange("(c p) n -> p c n", p=P)).then_inc(d_ff, 16)
                sp.dma_start(W2[0:last[1], NF - 1, :], w2[l][last[0]:FF, :]).then_inc(d_ff, 16)
                sp.dma_start(W2[last[1]:last[1] + 1, NF - 1, :], b2[l].unsqueeze(0)).then_inc(d_ff, 16)
                for half in range(2):
                    sp.dma_start(b1s[:, half, 0:NF - 1],
                                 b1[l][half * FF:half * FF + last[0]].rearrange("(c p) -> p c", p=P),
                                 allow_slow_non_contiguous=True).then_inc(d_ff, 16)
                    sp.dma_start(b1s[0:last[1], half, NF - 1:NF],
                                 b1[l][half * FF + last[0]:(half + 1) * FF].unsqueeze(1)).then_inc(d_ff, 16)

            load_scales(0)
            load_qkv(0)
            load_wo(0)
            load_ln(0)
            load_ff(0)
            with sp.Fori(0, DEPTH - 1) as L:
                sp.wait_ge(s_tab, 6 * L + 6)
                load_scales(L + 1)
                sp.wait_ge(s_pv, (L + 1) * SEQS * TILES)
                load_qkv(L + 1)
                sp.wait_ge(s_wo, (L + 1) * SEQS)
                load_wo(L + 1)
                sp.wait_ge(s_xne, (L + 1) * SEQS)
                load_ln(L + 1)
                sp.wait_ge(s_y, (L + 1) * SEQS)
                load_ff(L + 1)
            for q in range(4):
                sp.wait_ge(s_fin, q + 1)
                b = slice(q * SEQS // 4, (q + 1) * SEQS // 4)
                t = slice(q * SEQS * TILES // 4, (q + 1) * SEQS * TILES // 4)
                sp.dma_start(out[b].rearrange("b (t p) e -> p (b t) e", p=P), x1[:, t, :]).then_inc(d_out, 16)
            sp.wait_ge(d_out, 64)

        @block.gpsimd
        def _(pool):
            pool.memset(Vp[:, :, :, :], 0.0).then_inc(i_zero, 1)
            pool.wait_ge(i_zero, 1)
            pool.memset(Vp[:, :, :, DA:DA + 1], 1.0).then_inc(i_zero, 1)
            pool.memset(Wap[:, :, :], 0.0).then_inc(i_pad, 1)
            pool.memset(H[:, :, :], 1.0).then_inc(i_pad, 1)
            pool.memset(kbd[:, :, :, :], 0.0).then_inc(i_zero, 1)
            pool.memset(BD[:, :, :, :], 0.0).then_inc(i_zero, 1)
            pool.memset(xsT[:, :], 0.0).then_inc(i_zero, 1)
            pool.memset(x2T[:, :], 0.0).then_inc(i_zero, 1)
            pool.wait_ge(d_c, 16 * N_CONST)

            def spread_k(n):
                need(pool, a_ke, n + 1)
                need(pool, a_s, 4 * n)
                pool.tensor_tensor(KM[:, :, :], AkT[:, :].unsqueeze(1).broadcast_to([P, HA, SEQ]),
                                   headmask[:, :].unsqueeze(2).broadcast_to([P, HA, SEQ]), ALU.mult).then_inc(a_km, 1)

            spread_k(0)
            with pool.Fori(1, SEQS) as n:
                spread_k(pool.snap(n))
            pool.wait_ge(s_x, SEQS)

            def make_tables(l):
                pool.wait_ge(d_qks, 32 * l + 32)
                need(pool, s_ak, l * (SEQS * TILES))
                h = DH // 2
                for j in range(2):
                    sc = qks[:, j, :].unsqueeze(1).broadcast_to([P, TILES, DH])
                    pool.tensor_tensor(tab[:, :, 2 * j, :], rot[:, :, 2 * j, :], sc, ALU.mult).then_inc(s_tab, 1)
                    pool.tensor_tensor(tab[:, :, 2 * j + 1, 0:h], rot[:, :, 2 * j + 1, 0:h], sc[:, :, h:DH],
                                       ALU.mult).then_inc(s_tab, 1)
                    pool.tensor_tensor(tab[:, :, 2 * j + 1, h:DH], rot[:, :, 2 * j + 1, h:DH], sc[:, :, 0:h],
                                       ALU.mult).then_inc(s_tab, 1)
                pool.wait_ge(s_tab, 6 * l + 6)

            def stage_x(n, u):
                need(pool, s_xt, n)
                need_apart(pool, i_pool, s_x, n + 1)
                pool.tensor_copy(xst[:, :, :], xres[:, unit(u, 0), :]).then_inc(s_st, 1)

            def keep_x2(n, u):
                need_apart(pool, i_pool, s_r1, n)
                pool.tensor_copy(xres[:, unit(u, 1), :], x2s[:, :, :]).then_inc(s_xc, 1)

            def rotate(n, t, j):
                T = 2 * n + t
                col = slice(j * INNER, (j + 1) * INNER)
                h = DH // 2
                q4 = QH[:, col].rearrange("p (h d) -> p h d", d=DH)
                b4 = BQ[:, col].rearrange("p (h d) -> p h d", d=DH)
                s4 = tab[:, t, 2 * j + 1, :].unsqueeze(1).broadcast_to([P, HEADS, DH])
                need(pool, (s_qh, s_kh)[j], T + 1)
                pool.tensor_tensor(b4[:, :, 0:h], q4[:, :, h:DH], s4[:, :, 0:h], ALU.mult).then_inc((s_bq, s_bk)[j], 1)
                pool.tensor_tensor(b4[:, :, h:DH], q4[:, :, 0:h], s4[:, :, h:DH], ALU.mult).then_inc((s_bq, s_bk)[j], 1)
                need(pool, (s_bq, s_bk)[j], 2 * T + 2)
                need(pool, (s_aq, s_ak)[j], T + 1)
                pool.tensor_tensor(AQ[t][:, col], AQ[t][:, col], BQ[:, col], ALU.add).then_inc(s_rot, 1)

            def normalise(n, t):
                T = 2 * n + t
                need(pool, s_rl, T + 1)
                p3 = Pr[:, t, :].rearrange("p (h k) -> p h k", h=HEADS)
                pool.tensor_tensor(p3, p3, lsum[:, 1, :].unsqueeze(2).broadcast_to([P, HEADS, 2 * WIN]),
                                   ALU.mult).then_inc(s_pn, 1)

            def step(n, u, head, mid, ffn, layer):
                if head:
                    if isinstance(u, int) and u == 0:
                        make_tables(0 if isinstance(n, int) else layer + 1)
                    stage_x(n, u)
                if mid:
                    normalise(n - 1, 1)
                if head:
                    rotate(n, 0, 0)
                    rotate(n, 0, 1)
                    rotate(n, 1, 0)
                    rotate(n, 1, 1)
                if mid:
                    keep_x2(n, u)
                if head:
                    normalise(n, 0)

            stack_steps(pool, step)

        @block.scalar
        def _(act):
            act.preload_act_table_set(TABLE_SET)

            def rsqrt_guess(n, ready, lsem, done):
                need(act, ready, 3 * n + 3)
                act.activation(lw[:, 1, :], lw[:, 0, :], ACT.Ln).then_inc(lsem, 1)
                need(act, lsem, 2 * n + 1)
                act.activation(lw[:, 2, :], lw[:, 1, :], ACT.Exp, scale=-0.5).then_inc(lsem, 1)

            def a_head(n):
                rsqrt_guess(n, a_lnc, a_lnr, a_lnr)
                need(act, a_xt, n + 1)
                need(act, a_v, n)
                act.activation(xhT[:, :], TR[0][:, 0:SEQ], ACT.Copy).then_inc(a_xe, 1)
                need(act, a_qk, n + 1)
                need(act, a_s, 4 * n)
                act.activation(AqT[:, :], TR[1][:, 0:SEQ], ACT.Copy).then_inc(a_qe, 1)
                need(act, a_km, n)
                act.activation(AkT[:, :], TR[1][:, SEQ:2 * SEQ], ACT.Copy).then_inc(a_ke, 1)

            def a_values(n):
                need(act, a_v, n + 1)
                need(act, a_pv, n)
                act.activation(Vp[:, :, :, 0:DA],
                               TR[0][:, 0:SEQ].rearrange("p (t h d) -> p t h d", t=TILES, d=DA), ACT.Copy).then_inc(a_ve, 1)

            def a_exp(n, g):
                if g == 0:
                    need(act, a_t, 12 * n)
                need(act, a_nm, 4 * n + g + 1)
                bank = 3 * (g % 2)
                for h in range(4 * g, 4 * g + 4):
                    k = h - 4 * g
                    act.activation(E0[:, h, :], ps[:, bank, k * P:(k + 1) * P], ACT.Exp,
                                   bias=nmx[:, 1, 0, h:h + 1], scale=A_SCALE)
                    last = act.activation(E1[:, h, :], ps[:, bank + 1 + k // 2, (k % 2) * SEQ:(k % 2 + 1) * SEQ], ACT.Exp,
                                          bias=nmx[:, 1, 1, h:h + 1], scale=A_SCALE)
                last.then_inc(a_e, 1)

            def x1_norm(n):
                rsqrt_guess(n, b_lnc, b_lnr, b_lnr)

            def a_step(n, head, mid):
                if mid:
                    for g in range(4):
                        a_exp(n - 1, g)
                if head:
                    a_head(n)
                if head:
                    a_values(n)
                if mid:
                    x1_norm(n - 1)

            act.wait_ge(i_zero, 2)
            a_step(0, True, False)
            a_step(1, True, True)
            with act.Fori(2, SEQS) as n:
                a_step(act.snap(n), True, True)
            a_step(SEQS, False, True)
            act.wait_ge(s_x, SEQS)
            act.wait_ge(i_zero, 6)

            def evac_shifted(dst, sem, n, tr):
                h = DIM // 2
                act.activation(dst[0:h, 0:SEQ], tr[0:h, 0:SEQ], ACT.Copy)
                act.activation(dst[h:DIM, 1:SEQ + 1], tr[h:DIM, 0:SEQ], ACT.Copy).then_inc(sem, 1)

            def x_evac(n):
                need(act, s_xt, n + 1)
                need(act, s_pv, 2 * n)
                evac_shifted(xsT, s_xe, n, TR[0])

            def exps(n, t):
                T = 2 * n + t
                need(act, s_sub, T + 1)
                act.activation(Pr[:, t, :], Pr[:, t, :], ACT.Exp).then_inc(s_exp, 1)

            def gelus(n, chunks):
                for c in chunks:
                    m = FCH[c][1]
                    need(act, s_h, 3 * n + c + 1)
                    act.activation(G[0:m, c, :], TR[(c + 1) % 2][0:m, SEQ:2 * SEQ], ACT.Gelu,
                                   bias=b1s[0:m, 1, c:c + 1]).then_inc(s_gl, 1)

            def squares(n, t):
                T = 2 * n + t
                need(act, s_pq, T + 1)
                need(act, s_rq, T)
                act.activation(SQ[:, 0:INNER], PJ[t * 0][:, :], ACT.Square).then_inc(s_sqq, 1)
                need(act, s_pk, T + 1)
                need(act, s_rk, T)
                act.activation(SQ[:, INNER:2 * INNER], PJ[1][:, :], ACT.Square).then_inc(s_sqk, 1)

            def norm_guess(n, t):
                T = 2 * n + t
                need(act, s_fl, T + 1)
                act.activation(ss[:, 2, :], ss[:, 1, :], ACT.Ln).then_inc(s_lg, 1)
                need(act, s_lg, T + 1)
                act.activation(ss[:, 3, :], ss[:, 2, :], ACT.Exp, scale=-0.5).then_inc(s_iv, 1)

            def v_evac(n, t):
                T = 2 * n + t
                need(act, s_pv, T + 1)
                need(act, s_o, 2 * 2 * n)
                act.activation(V[:, t, :], PJ[t][:, :], ACT.Copy).then_inc(s_ve, 1)

            def qk_evac(n, t, groups):
                T = 2 * n + t
                for g in groups:
                    tr = TR[(g + t) % 2][:, :].rearrange("p (c n) -> p c n", c=4)
                    need(act, s_tr, 4 * T + g + 1)
                    need(act, s_sc, T)
                    c = slice(4 * (g % 2), 4 * (g % 2) + 4)
                    if g < 2:
                        act.activation(qT[:, c, :], tr, ACT.Copy).then_inc(s_te, 1)
                    else:
                        at = slice(WIN + P * t, WIN + P * t + P)
                        act.activation(kbd[0:DH, c, 0, at], tr[0:DH], ACT.Copy)
                        act.activation(kbd[DH:P, c, 1, at], tr[DH:P], ACT.Copy).then_inc(s_te, 1)

            def band_prev(n, t):
                T = 2 * n + t
                need(act, s_T, T + 1)
                need(act, s_o, 2 * T - 2)
                for w in range(NWIN):
                    src = PTr[32 * w:32 * w + 32, :, 0, :]
                    if w:
                        last = act.activation(BD[32 * w - 32:32 * w, t, :, 32 * w:32 * w + 32], src, ACT.Copy)
                    elif t:
                        act.activation(BB[P - WIN:P, :, :], src, ACT.Copy)
                last.then_inc(s_bdp, 1)

            def o_evac_b(n):
                for g in range(2):
                    need(act, s_o, 4 * n + g + 3)
                    need(act, s_oe, 4 * n + 2)
                    act.activation(oT[:, 1, 4 * g:4 * g + 4, :], (TR[1], SC[:, 0, :])[g].rearrange("p (c n) -> p c n", c=4),
                                   ACT.Copy).then_inc(s_oe, 1)

            def x2_evac(n):
                need(act, s_x2, n + 1)
                need(act, s_bk2, n)
                evac_shifted(x2T, s_x2e, n, TR[0])

            def xn_evac(n, layer_wait):
                need(act, s_xn, n + 1)
                need(act, s_h, 3 * n)
                act.wait_ge(d_ln, layer_wait)
                act.activation(xnT[:, :], TR[0][:, 0:SEQ], ACT.Identity, bias=lnb[:, :], scale=lng[:, :]).then_inc(s_xne, 1)

            def step(n, u, head, mid, ffn, layer):
                first = isinstance(u, int) and not isinstance(n, int)
                if head:
                    x_evac(n)
                if mid:
                    exps(n - 1, 1)
                    band_prev(n - 1, 0)
                if ffn:
                    act.wait_ge(d_ff, 16 * N_FF * (layer + 1))
                    gelus(n - 2, range(NF - 1))
                if head:
                    squares(n, 0)
                if ffn:
                    gelus(n - 2, (NF - 1,))
                    act.preload_act_table_set(TABLE_SET)
                if mid:
                    band_prev(n - 1, 1)
                if head:
                    norm_guess(n, 0)
                if mid:
                    o_evac_b(n - 1)
                if head:
                    squares(n, 1)
                    qk_evac(n, 0, (0, 1))
                    norm_guess(n, 1)
                    qk_evac(n, 0, (2, 3))
                    v_evac(n, 0)
                    exps(n, 0)
                    v_evac(n, 1)
                if mid:
                    x2_evac(n - 1)
                if head:
                    qk_evac(n, 1, range(4))
                if mid:
                    rsqrt_guess(n - 1, s_lnc, s_lnr, s_lnr)
                if mid:
                    later = layer + 1 if first and u == 1 else layer
                    xn_evac(n - 1, 32 * (later + 1))

            stack_steps(act, step)

        @block.vector
        def _(dve):
            def moments(n, chain, src):
                for t in range(TILES):
                    last = dve.bn_stats(stats[:, t, :], src[:, t, :])
                last.then_inc(chain, 1)
                need_apart(dve, i_dve, chain, 3 * n + 1)
                for t in range(TILES):
                    last = dve.bn_aggr(mv[:, t, :], stats[:, t, :])
                last.then_inc(chain, 1)
                dve.wait_ge(chain, 3 * n + 2)
                dve.tensor_scalar(lw[:, 0, :], mv[:, :, 1], EPS, None, ALU.add).then_inc(chain, 1)

            def newton(n, k, v, y0, t1, y1, chain):
                dve.tensor_tensor(t1, y0, y0, ALU.mult).then_inc(chain, 1)
                dve.wait_ge(chain, 4 * n + 1)
                dve.tensor_tensor(t1, t1, v, ALU.mult).then_inc(chain, 1)
                dve.wait_ge(chain, 4 * n + 2)
                dve.tensor_scalar(t1, t1, -0.5, 1.5, ALU.mult, ALU.add).then_inc(chain, 1)
                dve.wait_ge(chain, 4 * n + 3)
                dve.tensor_tensor(y1, y0, t1, ALU.mult).then_inc(chain, 1)
                dve.wait_ge(chain, 4 * n + 4)

            def normalised(n, dst, src, rsem, nsem, done):
                need(dve, rsem, 2 * n + 2)
                newton(n, TILES, lw[:, 0, :], lw[:, 2, :], lw[:, 3, :], lw[:, 4, :], nsem)
                for t in range(TILES):
                    last = dve.tensor_scalar(dst[:, t, :], src[:, t, :], mv[:, t, 0:1], lw[:, 4, t:t + 1],
                                             ALU.subtract, ALU.mult)
                last.then_inc(done, 1)

            dve.wait_ge(d_c, 16 * N_CONST)
            dve.tensor_copy(ident_h[:, :], ident[:, :]).then_inc(i_const, 1)
            dve.tensor_copy(causal[:, :], causal_f[:, :]).then_inc(i_const, 1)
            dve.tensor_copy(wmask[:, :, :], wmask_f[:, :, :]).then_inc(i_const, 1)
            dve.wait_ge(d_x, 16)

            def a_norm(n):
                un = slice(n * TILES, n * TILES + TILES) if isinstance(n, int) else bass.ds(n * TILES, TILES)
                xt = xres[:, un, :]
                moments(n, a_lnc, xt)
                need(dve, a_xt, n)
                normalised(n, xh, xt, a_lnr, a_lnn, a_xh)

            def a_max(n, g):
                bank = 3 * (g % 2)
                need(dve, a_s, 4 * n + g + 1)
                if g == 0:
                    need(dve, a_e, 4 * n)
                hs = slice(4 * g, 4 * g + 4)
                dve.tensor_reduce(nmx[:, 0, 0, hs], ps[:, bank, :].rearrange("p (h k) -> p h k", h=4), AX.X, ALU.max)
                dve.tensor_reduce(nmx[:, 0, 1, hs], ps[:, bank + 1:bank + 3, :].rearrange("p a (h k) -> p (a h) k", h=2),
                                  AX.X, ALU.max).then_inc(a_mx, 1)
                need(dve, a_mx, 4 * n + g + 1)
                dve.tensor_scalar(nmx[:, 1, :, hs], nmx[:, 0, :, hs], -A_SCALE, None, ALU.mult).then_inc(a_nm, 1)

            def a_evac(n, g):
                if g == 0:
                    need(dve, a_pv, n)
                for j in range(3):
                    i = 3 * g + j
                    slot = (i + (0 if i < 6 else 0)) % 2
                    need(dve, a_t, 12 * n + i + 1)
                    src = TR[slot][:, :].rearrange("p (h q) -> p h q", h=4)
                    dst = (PT0[:, 4 * g:4 * g + 4, 0:P], PT0[:, 4 * g:4 * g + 4, P:SEQ], PT1[:, 4 * g:4 * g + 4, :])[j]
                    dve.tensor_copy(dst, src).then_inc(a_te, 1)

            def a_divide(n):
                need(dve, a_pv, n + 1)
                dve.transpose(AoT[:, :], ps[:, 0:2, :].rearrange("p a q -> p (a q)")).then_inc(a_oe, 1)
                need(dve, a_oe, n + 1)
                o3 = AoT[:, :].rearrange("p (b r) -> p b r", r=32)
                dve.reciprocal(Arl[:, :], o3[:, :, DA]).then_inc(a_rc, 1)
                need(dve, a_rc, n + 1)
                dve.tensor_tensor(o3, o3, Arl[:, :].unsqueeze(2).broadcast_to([P, 32, 32]), ALU.mult).then_inc(a_mu, 1)
                need(dve, a_mu, n + 1)
                need(dve, a_wo, n)
                dve.transpose(AoN[:, :, :].rearrange("p c q -> p (c q)"), AoT[:, :]).then_inc(a_on, 1)

            def a_residual(n):
                un = bass.ds(n * TILES, TILES) if not isinstance(n, int) else slice(n * TILES, n * TILES + TILES)
                need(dve, a_wo, n + 1)
                dve.tensor_tensor(x1[:, un, :], ps[:, 5, 0:SEQ].rearrange("p (t e) -> p t e", t=TILES), xres[:, un, :],
                                  ALU.add).then_inc(a_x1, 1)
                need_apart(dve, i_dve, a_x1, n + 1)
                moments(n, b_lnc, x1[:, un, :])
                normalised(n, xres[:, un, :], x1[:, un, :], b_lnr, b_lnn, s_x)

            def a_step(n, head, mid):
                if mid:
                    a_max(n - 1, 0)
                    a_max(n - 1, 1)
                    a_evac(n - 1, 0)
                    a_max(n - 1, 2)
                    a_evac(n - 1, 1)
                    a_max(n - 1, 3)
                if head:
                    a_norm(n)
                if mid:
                    a_evac(n - 1, 2)
                    a_evac(n - 1, 3)
                    a_divide(n - 1)
                    a_residual(n - 1)

            a_step(0, True, False)
            a_step(1, True, True)
            with dve.Fori(2, SEQS) as n:
                a_step(dve.snap(n), True, True)
            a_step(SEQS, False, True)

            def soft_max(n, t):
                T = 2 * n + t
                s3 = SC.rearrange("p a (h k) -> p (a h) k", k=2 * WIN)
                need(dve, s_sc, T + 1)
                dve.tensor_reduce(mx[:, :], s3, AX.X, ALU.max).then_inc(s_mx, 1)
                need(dve, s_mx, T + 1)
                dve.tensor_tensor(Pr[:, t, :].rearrange("p (h k) -> p h k", h=HEADS), s3,
                                  mx[:, :].unsqueeze(2).broadcast_to([P, HEADS, 2 * WIN]), ALU.subtract).then_inc(s_sub, 1)

            def soft_sum(n, t):
                T = 2 * n + t
                need(dve, s_exp, T + 1)
                dve.tensor_reduce(lsum[:, 0, :], Pr[:, t, :].rearrange("p (h k) -> p h k", h=HEADS), AX.X, ALU.add).then_inc(s_sum, 1)
                need(dve, s_sum, T + 1)
                need(dve, s_pn, T)
                dve.reciprocal(lsum[:, 1, :], lsum[:, 0, :]).then_inc(s_rl, 1)

            def turn(n, t):
                T = 2 * n + t
                need(dve, s_pn, T + 1)
                need(dve, s_bdp, T)
                dve.transpose(PTr[:, :, :, :].rearrange("p h b i -> p (h b i)"), Pr[:, t, :]).then_inc(s_T, 1)
                need(dve, s_T, T + 1)
                need(dve, s_o, 2 * T - 2)
                for w in range(NWIN):
                    rows = slice(32 * w, 32 * w + 32)
                    last = dve.tensor_copy(BD[rows, t, :, rows], PTr[rows, :, 1, :])
                last.then_inc(s_bdc, 1)

            def gated(n, chunks):
                for c in chunks:
                    m = FCH[c][1]
                    need(dve, s_gl, 3 * n + c + 1)
                    dve.scalar_tensor_tensor(H[0:m, c, :], TR[(c + 1) % 2][0:m, 0:SEQ], b1s[0:m, 0, c:c + 1],
                                             G[0:m, c, :], ALU.add, ALU.mult).then_inc(s_g, 1)

            def sum_q(n, t):
                T = 2 * n + t
                need(dve, s_sqq, T + 1)
                dve.tensor_reduce(ss[:, 0, 0:HEADS], SQ[:, 0:INNER].rearrange("p (h d) -> p h d", d=DH), AX.X, ALU.add).then_inc(s_rq, 1)

            def sum_k(n, t):
                T = 2 * n + t
                need(dve, s_sqk, T + 1)
                dve.tensor_reduce(ss[:, 0, HEADS:], SQ[:, INNER:].rearrange("p (h d) -> p h d", d=DH), AX.X, ALU.add).then_inc(s_rk, 1)
                need(dve, s_rk, T + 1)
                dve.tensor_scalar(ss[:, 1, :], ss[:, 0, :], NORM_FLOOR * NORM_FLOOR, None, ALU.max).then_inc(s_fl, 1)

            def over_norms(n, t):
                T = 2 * n + t
                need(dve, s_iv, T + 1)
                newton(T, 2 * HEADS, ss[:, 1, :], ss[:, 3, :], ss[:, 4, :], inv[:, :], s_nw)
                for j in range(2):
                    col = slice(j * INNER, (j + 1) * INNER)
                    need(dve, (s_bq, s_bk)[j], 2 * T)
                    dve.tensor_tensor(QH[:, col].rearrange("p (h d) -> p h d", d=DH),
                                      PJ[j][:, :].rearrange("p (h d) -> p h d", d=DH),
                                      inv[:, j * HEADS:(j + 1) * HEADS].unsqueeze(2).broadcast_to([P, HEADS, DH]),
                                      ALU.mult).then_inc((s_qh, s_kh)[j], 1)
            def cosines(n, t):
                T = 2 * n + t
                for j in range(2):
                    col = slice(j * INNER, (j + 1) * INNER)
                    need(dve, (s_qh, s_kh)[j], T + 1)
                    need(dve, s_tr, 4 * T - 6 + 2 * j)
                    dve.tensor_tensor(AQ[t][:, col].rearrange("p (h d) -> p h d", d=DH),
                                      QH[:, col].rearrange("p (h d) -> p h d", d=DH),
                                      tab[:, t, 2 * j, :].unsqueeze(1).broadcast_to([P, HEADS, DH]),
                                      ALU.mult).then_inc((s_aq, s_ak)[j], 1)

            def residual2(n, u):
                need(dve, s_y, n + 1)
                need(dve, s_xc, n + 1)
                xr = xres[:, unit(u, 2), :]
                dve.tensor_tensor(xr, TR[0][:, 0:SEQ].rearrange("p (t e) -> p t e", t=TILES), xr, ALU.add).then_inc(s_x, 1)

            def o_evac_a(n):
                for g in range(2):
                    need(dve, s_o, 4 * n + g + 1)
                    need(dve, s_wo, n)
                    dve.tensor_copy(oT[:, 0, 4 * g:4 * g + 4, :],
                                    SC[:, g, :].rearrange("p (c n) -> p c n", c=4)).then_inc(s_oe, 1)

            def residual1(n, u):
                need(dve, s_wo, n + 1)
                need(dve, s_xc, n)
                dve.tensor_tensor(x2s[:, :, :], SC[:, 1, 0:SEQ].rearrange("p (t e) -> p t e", t=TILES),
                                  xres[:, unit(u, 1), :], ALU.add).then_inc(s_r1, 1)

            def layer_norm(n):
                src = TR[1][:, 0:SEQ].rearrange("p (t e) -> p t e", t=TILES)
                need_apart(dve, i_dve, s_bk2, n + 1)
                moments(n, s_lnc, src)
                need(dve, s_xn, n)
                normalised(n, xn, src, s_lnr, s_lnn, s_ln)

            def step(n, u, head, mid, ffn, layer):
                if mid:
                    soft_max(n - 1, 1)
                    turn(n - 1, 0)
                    soft_sum(n - 1, 1)
                if ffn:
                    gated(n - 2, range(NF - 1))
                if head:
                    sum_q(n, 0)
                if ffn:
                    gated(n - 2, (NF - 1,))
                if mid:
                    turn(n - 1, 1)
                    o_evac_a(n - 1)
                if head:
                    sum_k(n, 0)
                if ffn:
                    residual2(n - 2, u)
                if head:
                    over_norms(n, 0)
                if head:
                    if isinstance(u, int) and u == 0:
                        dve.wait_ge(s_tab, 6 if isinstance(n, int) else 6 * layer + 12)
                    cosines(n, 0)
                if mid:
                    residual1(n - 1, u)
                if head:
                    sum_q(n, 1)
                    sum_k(n, 1)
                    over_norms(n, 1)
                    cosines(n, 1)
                    soft_max(n, 0)
                    soft_sum(n, 0)
                if mid:
                    layer_norm(n - 1)

            stack_steps(dve, step)
            dve.wait_ge(s_x, (DEPTH + 1) * SEQS)
            for q in range(4):
                t = slice(q * SEQS * TILES // 4, (q + 1) * SEQS * TILES // 4)
                dve.tensor_tensor(x1[:, t, :], x1[:, t, :], xres[:, t, :], ALU.add).then_inc(s_fin, 1)

        @block.tensor
        def _(pe):
            mm, tp = pe.matmul, pe.transpose

            def a_turn(n):
                need(pe, a_xh, n + 1)
                for t in range(TILES):
                    last = tp(TR[0][:, t * P:(t + 1) * P], xh[:, t, :], ident[:, :])
                last.then_inc(a_xt, 1)

            def a_project(n):
                need(pe, a_xe, n + 1)
                for i in range(2):
                    last = mm(TR[1][:, i * SEQ:(i + 1) * SEQ], Wa[:, i, :], xhT[:, :], start=True, stop=True)
                last.then_inc(a_qk, 1)

            def a_project_v(n):
                for t in range(TILES):
                    last = mm(TR[0][:, t * P:(t + 1) * P], xhT[:, t * P:(t + 1) * P], Wa[:, 2, :], start=True, stop=True)
                last.then_inc(a_v, 1)

            def a_scores(n, g):
                bank = 3 * (g % 2)
                if g == 0:
                    need(pe, a_km, n + 1)
                    need(pe, a_qe, n + 1)
                    need(pe, a_oe, n)
                if g == 1:
                    need(pe, a_x1, n)
                if g >= 2:
                    need(pe, a_e, 4 * n + g - 1)
                mm(ps[:, bank, :], ident_h[:, :], causal[:, P:2 * P].unsqueeze(1).broadcast_to([P, 4, P]),
                   start=True, stop=False, skip_group_check=True)
                for b in range(2):
                    mm(ps[:, bank + 1 + b, :], ident_h[:, :], causal[:, :].unsqueeze(1).broadcast_to([P, 2, SEQ]),
                       start=True, stop=False, skip_group_check=True)
                for k in range(4):
                    h = 4 * g + k
                    mm(ps[:, bank, k * P:(k + 1) * P], AqT[:, 0:P], KM[:, h, 0:P],
                       start=False, stop=True, skip_group_check=True)
                for k in range(4):
                    h = 4 * g + k
                    last = mm(ps[:, bank + 1 + k // 2, (k % 2) * SEQ:(k % 2 + 1) * SEQ], AqT[:, P:SEQ], KM[:, h, :],
                              start=False, stop=True, skip_group_check=True)
                last.then_inc(a_s, 1)

            def a_transposes(n, g):
                need(pe, a_e, 4 * n + g + 1)
                for j in range(3):
                    i = 3 * g + j
                    if i < 2:
                        need(pe, a_ve, n + 1)
                    elif i in (6, 7):
                        need(pe, a_te, 12 * n + i)
                        if i == 7:
                            need(pe, a_ke, n + 2)
                        else:
                            need(pe, a_xe, n + 2)
                    else:
                        need(pe, a_te, 12 * n + i - 1)
                    for k in range(4):
                        h = 4 * g + k
                        src = (E0[:, h, :], E1[:, h, 0:P], E1[:, h, P:SEQ])[j]
                        last = tp(TR[i % 2][:, k * P:(k + 1) * P], src, ident[:, :])
                    last.then_inc(a_t, 1)

            def a_values(n):
                need(pe, a_te, 12 * n + 12)
                for c in range(4):
                    for g in range(4):
                        h = 4 * c + g
                        o = ps[32 * g:32 * g + 32, c // 2, (c % 2) * SEQ:(c % 2 + 1) * SEQ]
                        mm(o, Vp[:, 0, h, :], PT0[:, h, :], start=(c % 2 == 0), stop=False, skip_group_check=True)
                for c in range(4):
                    for g in range(4):
                        h = 4 * c + g
                        o = ps[32 * g:32 * g + 32, c // 2, (c % 2) * SEQ + P:(c % 2 + 1) * SEQ]
                        last = mm(o, Vp[:, 1, h, :], PT1[:, h, :], start=False, stop=True, skip_group_check=True)
                last.then_inc(a_pv, 1)

            def a_output(n):
                need(pe, a_on, n + 1)
                for t in range(TILES):
                    for c in range(4):
                        last = mm(ps[:, 5, t * P:(t + 1) * P], AoN[:, c, t * P:(t + 1) * P], Wap[:, c, :],
                                  start=(c == 0), stop=(c == 3))
                last.then_inc(a_wo, 1)

            def a_step(n, head, mid):
                if mid:
                    a_scores(n - 1, 0)
                    a_scores(n - 1, 1)
                    a_transposes(n - 1, 0)
                    a_scores(n - 1, 2)
                    a_transposes(n - 1, 1)
                    a_scores(n - 1, 3)
                if head:
                    if mid:
                        need(pe, a_te, 12 * n - 12 + 6)
                    a_turn(n)
                    a_project(n)
                if mid:
                    if not head:
                        a_tail_transposes(n - 1)
                    else:
                        a_transposes(n - 1, 2)
                        a_transposes(n - 1, 3)
                    a_values(n - 1)
                if head:
                    if mid:
                        need(pe, a_te, 12 * n)
                    a_project_v(n)
                if mid:
                    a_output(n - 1)

            def a_tail_transposes(n):
                for g in (2, 3):
                    need(pe, a_e, 4 * n + g + 1)
                    for j in range(3):
                        i = 3 * g + j
                        need(pe, a_te, 12 * n + i - 1)
                        for k in range(4):
                            h = 4 * g + k
                            src = (E0[:, h, :], E1[:, h, 0:P], E1[:, h, P:SEQ])[j]
                            last = tp(TR[i % 2][:, k * P:(k + 1) * P], src, ident[:, :])
                        last.then_inc(a_t, 1)

            pe.wait_ge(d_c, 16 * N_CONST)
            pe.wait_ge(i_const, 3)
            pe.wait_ge(d_wa, 16 * N_WA)
            a_step(0, True, False)
            a_step(1, True, True)
            with pe.Fori(2, SEQS) as n:
                a_step(pe.snap(n), True, True)
            a_step(SEQS, False, True)
            pe.wait_ge(s_x, SEQS)

            def turn_x(n):
                need(pe, s_st, n + 1)
                need(pe, s_xne, n - 1)
                for t in range(TILES):
                    last = tp(TR[0][:, t * P:(t + 1) * P], xst[:, t, :], ident[:, :])
                last.then_inc(s_xt, 1)

            def hidden(n, chunks, head):
                need(pe, s_xne, n + 1)
                for c in chunks:
                    f0, m = FCH[c]
                    if c == 0:
                        need(pe, s_ln, n + 1)
                    if c == 1 and head:
                        need(pe, s_xe, n + 3)
                    if c == 2:
                        need(pe, s_g, 3 * n + 1)
                    for half in range(2):
                        last = mm(TR[(c + 1) % 2][0:m, half * SEQ:(half + 1) * SEQ],
                                  W1[:, half * FF + f0:half * FF + f0 + m], xnT[:, :], start=True, stop=True)
                    last.then_inc(s_h, 1)

            def project(n, t):
                T = 2 * n + t
                need(pe, s_xe, n + 1)
                xt = xsT[:, t * P:(t + 1) * P]
                if t == 0:
                    need(pe, s_ve, T - 1)
                else:
                    need(pe, s_qh, T)
                for b in range(2):
                    last = mm(PJ[0][:, b * 512:(b + 1) * 512], xt, Wqkv[:, b * 512:(b + 1) * 512], start=True, stop=True)
                last.then_inc(s_pq, 1)
                if t == 0:
                    need(pe, s_ve, T)
                else:
                    need(pe, s_kh, T)
                for b in range(2):
                    last = mm(PJ[1][:, b * 512:(b + 1) * 512], xt, Wqkv[:, INNER + b * 512:INNER + (b + 1) * 512],
                              start=True, stop=True)
                last.then_inc(s_pk, 1)

            def project_v(n, t):
                need(pe, (s_qh, s_kh)[t], 2 * n + 2)
                xt = xsT[:, t * P:(t + 1) * P]
                for b in range(2):
                    last = mm(PJ[t][:, b * 512:(b + 1) * 512], xt, Wqkv[:, 2 * INNER + b * 512:2 * INNER + (b + 1) * 512],
                              start=True, stop=True)
                last.then_inc(s_pv, 1)

            def values(n, t):
                T = 2 * n + t
                need(pe, s_bdc, T + 1)
                need(pe, s_bdp, T + 1)
                need(pe, s_ve, T + 1)
                for g in range(2):
                    slot = (SC[:, g, :], (TR[1], SC[:, 0, :])[g])[t]
                    if t == 0 and g == 0:
                        need(pe, s_sub, T + 2)
                    if t == 1 and g == 1:
                        need(pe, s_oe, 4 * n + 1)
                    for c in range(4):
                        for k in range(2):
                            h = 2 * (4 * g + c) + k
                            last = mm(slot[DH * k:DH * k + DH, c * P:(c + 1) * P], V[:, t, h * DH:(h + 1) * DH], BD[:, t, h, :],
                               start=(c == 0), stop=False, skip_group_check=True)
                    for c in range(4):
                        for k in range(2):
                            h = 2 * (4 * g + c) + k
                            if t:
                                last = mm(slot[DH * k:DH * k + DH, c * P:c * P + WIN],
                                          V[P - WIN:P, 0, h * DH:(h + 1) * DH], BB[P - WIN:P, h, :],
                                          start=False, stop=True, skip_group_check=True)
                    last.then_inc(s_o, 1)

            def output(n):
                for t in range(TILES):
                    need(pe, s_oe, 4 * n + 2 * t + 2)
                    for c in range(PAIRS):
                        last = mm(SC[:, 1, t * P:(t + 1) * P], oT[:, t, c, :], Wo[:, c, :],
                                  start=(c == 0), stop=(c == PAIRS - 1))
                last.then_inc(s_wo, 1)

            def turn_qk(n, t, ffn=False):
                T = 2 * n + t
                for g in range(4):
                    if g in (0, 2):
                        need(pe, s_rot, 2 * T + g // 2 + 1)
                    if g >= 2:
                        need(pe, s_te, 4 * T + g - 1)
                    elif t == 1:
                        if g == 0:
                            need(pe, s_te, 4 * T)
                        else:
                            need(pe, s_x2e, n)
                    elif g == 0 and ffn:
                        need(pe, s_x, SEQS + n - 1)
                    for c in range(4):
                        q0 = g * 512 + c * P
                        last = tp(TR[(g + t) % 2][:, c * P:(c + 1) * P], AQ[t][:, q0:q0 + P], ident[:, :])
                    last.then_inc(s_tr, 1)

            def scores(n, t, mid=False):
                T = 2 * n + t
                need(pe, s_te, 4 * T + 4)
                need(pe, s_sub, T)
                if mid:
                    need(pe, s_r1, n)
                for b in range(2):
                    mm(SC[:, b, :], ident_h[:, :], wmask[:, t, :].unsqueeze(1).broadcast_to([P, 8, 2 * WIN]),
                       start=True, stop=False, skip_group_check=True)
                for c in range(PAIRS):
                    for w in range(NWIN):
                        k0 = P * t + WIN * w
                        last = mm(SC[32 * w:32 * w + 32, c // 4, (c % 4) * P:(c % 4 + 1) * P],
                                  qT[:, c, 32 * w:32 * w + 32], kbd[:, c, :, k0:k0 + 2 * WIN],
                                  start=False, stop=True, skip_group_check=True)
                last.then_inc(s_sc, 1)

            def turn_x2(n, tail):
                need(pe, s_r1, n + 1)
                if tail:
                    need(pe, s_x, SEQS + n)
                for t in range(TILES):
                    last = tp(TR[0][:, t * P:(t + 1) * P], x2s[:, t, :], ident[:, :])
                last.then_inc(s_x2, 1)

            def turn_back(n, T):
                need(pe, s_x2e, n + 1)
                if T is not None:
                    need(pe, s_te, 4 * T + 3)
                for t in range(TILES):
                    last = tp(TR[1][:, t * P:(t + 1) * P], x2T[:, t * P:(t + 1) * P], ident[:, :])
                last.then_inc(s_bk2, 1)

            def turn_xn(n):
                need(pe, s_ln, n + 1)
                for t in range(TILES):
                    last = tp(TR[0][:, t * P:(t + 1) * P], xn[:, t, :], ident[:, :])
                last.then_inc(s_xn, 1)

            def feed_out(n):
                need(pe, s_g, 3 * n + 3)
                for t in range(TILES):
                    for c, (_, m) in enumerate(FCH):
                        k = m + (c == NF - 1)
                        last = mm(TR[0][:, t * P:(t + 1) * P], H[0:k, c, t * P:(t + 1) * P], W2[0:k, c, :],
                                  start=(c == 0), stop=(c == NF - 1))
                last.then_inc(s_y, 1)

            def step(n, u, head, mid, ffn, layer):
                if head:
                    turn_x(n)
                if ffn:
                    pe.wait_ge(d_ff, 16 * N_FF * (layer + 1))
                    hidden(n - 2, range(NF - 1), head)
                if head:
                    if isinstance(u, int) and u == 0:
                        pe.wait_ge(d_qkv, 16 if isinstance(n, int) else 16 * (layer + 2))
                    project(n, 0)
                if ffn:
                    hidden(n - 2, (NF - 1,), head)
                if mid:
                    values(n - 1, 0)
                if ffn:
                    feed_out(n - 2)
                if mid:
                    values(n - 1, 1)
                    if isinstance(u, int) and u == 1:
                        pe.wait_ge(d_wo, 16 if isinstance(n, int) else 16 * (layer + 2))
                    output(n - 1)
                if head:
                    project(n, 1)
                    turn_qk(n, 0, ffn)
                    scores(n, 0, mid)
                    project_v(n, 0)
                    project_v(n, 1)
                if mid:
                    turn_x2(n - 1, not head)
                if head:
                    turn_qk(n, 1)
                if mid:
                    turn_back(n - 1, 2 * n + 1 if head else None)
                if head:
                    scores(n, 1)
                if mid:
                    turn_xn(n - 1)

            stack_steps(pe, step)


def constants():
    import numpy as np
    f = np.float32
    low = f(-3.0e38)
    i = np.arange(P)
    win = np.zeros((P, 2, 2 * WIN), f)
    c = np.arange(2 * WIN)[None, :]
    r = (i % WIN)[:, None]
    hidden = (r < c - WIN) | (r > c)
    win[:, 0] = np.where(hidden | ((i[:, None] < WIN) & (c < WIN)), low, f(0))
    win[:, 1] = np.where(hidden, low, f(0))
    causal = np.zeros((P, 2 * P), f)
    causal[:, P:] = np.where(i[None, :] > i[:, None], low, f(0))
    headmask = (i[:, None] // DA == np.arange(HA)[None, :]).astype(f)
    half = np.arange(0, DH, 2, dtype=f)
    inv_freq = f(1.0) / f(10000.0) ** (half / f(DH))
    t = np.arange(SEQ, dtype=f)
    freqs = (t[:, None] * inv_freq[None, :]).astype(f)
    base = (half + f(0.4 * DH)) / f(1.4 * DH)
    scale = base[None, :] ** ((t - f(SEQ // 2)) / f(WIN // 2))[:, None]
    cos, sin = np.cos(freqs), np.sin(freqs)
    tabs = np.stack([np.concatenate([cos * scale, cos * scale], 1) * f(QK_SCALE),
                     np.concatenate([-sin * scale, sin * scale], 1) * f(QK_SCALE),
                     np.concatenate([cos / scale, cos / scale], 1),
                     np.concatenate([-sin / scale, sin / scale], 1)], 1).astype(f)
    rot = np.ascontiguousarray(tabs.reshape(TILES, P, 4, DH).transpose(1, 0, 2, 3))
    return [np.eye(P, dtype=f), win, causal, headmask, rot]


def kernel(**inputs):
    import numpy as _np
    import concourse.bacc as _bacc
    from concourse.bass_utils import run_bass_kernel_spmd as _run

    nc = _bacc.Bacc("TRN2", target_bir_lowering=False, num_devices=1)
    arrays, args = {}, []

    def give(name, a):
        a = _np.ascontiguousarray(a)
        arrays[name] = a
        args.append(nc.dram_tensor(name, a.shape, mybir.dt.from_np(a.dtype), kind="ExternalInput").ap())

    give("x", inputs["L0_attn_x"])
    for w in ("Wq", "Wk", "Wv", "Wo"):
        give(w + "_t", _np.asarray(inputs["L0_attn_" + w]).T)
    for w in ("Wqkv", "q_scale", "k_scale", "Wo", "ln_g", "ln_b", "W1", "b1", "W2", "b2"):
        give("ffn_" + w, inputs["L0_ffn_" + w])
    for i, a in enumerate(constants()):
        give(f"const_{i}", a)
    args.append(nc.dram_tensor("out_0", (SEQS, SEQ, DIM), F32, kind="ExternalOutput").ap())
    build(nc, *args)
    r = _run(nc, [arrays], core_ids=[0])
    return r.results[0]["out_0"]
```

```python
from contextlib import ExitStack

import concourse.bass as bass
from concourse import mybir

F32 = mybir.dt.float32
BF16 = mybir.dt.bfloat16
ALU = mybir.AluOpType
ACT = mybir.ActivationFunctionType
AX = mybir.AxisListType
P = 128

SEQS, SEQ, DIM = 16, 256, 128
TILES = SEQ // P
HA, DA = 16, 8
DEPTH, HEADS, DH = 6, 16, 64
INNER = HEADS * DH
PAIRS = HEADS // 2
WIN = 32
NWIN = P // WIN
FF = int(DIM * 4 * 2 / 3)
FCH = [(c, min(P, FF - c)) for c in range(0, FF, P)]
NF = len(FCH)
QK_SCALE = 8.0
A_SCALE = 1.0 / float(DA) ** 0.5
EPS = 1e-5
NORM_FLOOR = 1e-12
TABLE_SET = "natural_log_exp_and_others"


def need(eng, sem, value):
    if isinstance(value, int) and value <= 0:
        return
    eng.wait_ge(sem, value)


def need_apart(eng, idle, sem, value):
    need(eng, sem, value)
    eng.sem_inc(idle, 1)


def build(nc, x_in, wq_t, wk_t, wv_t, wo_t, wqkv, q_scale, k_scale, wo2, ln_g, ln_b, w1, b1, w2, b2,
          c_ident, c_winmask, c_causal, c_headmask, c_rot, out):
    with ExitStack() as ctx:
        def sb(name, shape, dt=F32):
            return ctx.enter_context(nc.sbuf_tensor(name, shape, dt))

        def sem(name):
            return ctx.enter_context(nc.semaphore(name))

        ps = ctx.enter_context(nc.psum_tensor("ps", [P, 8, 512], F32))

        xres = sb("xres", [P, SEQS * TILES, DIM])
        x1 = sb("x1", [P, SEQS * TILES, DIM])
        ident = sb("ident", [P, P])
        ident_h = sb("ident_h", [P, P], BF16)
        wmask_f = sb("wmask_f", [P, 2, 2 * WIN])
        wmask = sb("wmask", [P, 2, 2 * WIN], BF16)
        causal_f = sb("causal_f", [P, 2 * P])
        causal = sb("causal", [P, 2 * P], BF16)
        headmask = sb("headmask", [P, HA])
        rot = sb("rot", [P, TILES, 4, DH])
        Wqkv = sb("Wqkv", [P, 3 * INNER])
        Wo = sb("Wo", [P, PAIRS, DIM])
        W1 = sb("W1", [P, 2 * FF])
        W2 = sb("W2", [P, NF, DIM])
        lng = sb("lng", [P, 1])
        lnb = sb("lnb", [P, 1])
        b1s = sb("b1s", [P, 2, NF])
        qks = sb("qks", [P, 2, DH])
        tab = sb("tab", [P, TILES, 4, DH])
        area1 = sb("area1", [P, 3, 2048])
        SQ, QH = area1[:, 0, :], area1[:, 1, :]
        AQ = [area1[:, 2, :], sb("AQb", [P, 2048])[:, :]]
        E0 = area1[:, 0, :].rearrange("p (h k) -> p h k", h=HA)
        E1 = area1[:, 1:3, :].rearrange("p a k -> p (a k)").rearrange("p (h k) -> p h k", h=HA)
        area2 = sb("area2", [P, 4096])
        BQ = area2[:, 0:2048]
        V = area2[:, 2048:4096].rearrange("p (t n) -> p t n", t=TILES)
        PT0 = area2[:, :].rearrange("p (h q) -> p h q", h=HA)
        area3 = sb("area3", [P, 4096])
        Pr = area3[:, 0:2048].rearrange("p (t n) -> p t n", t=TILES)
        oT = area3[:, 2048:4096].rearrange("p (t c n) -> p t c n", t=TILES, c=PAIRS)
        KM = area3[:, :].rearrange("p (h k) -> p h k", h=HA)
        area4 = sb("area4", [P, 2048])
        PT1 = area4[:, :].rearrange("p (h q) -> p h q", h=HA)
        qT = area4[:, 0:1024].rearrange("p (c n) -> p c n", c=PAIRS)
        PTr = area4[:, 1024:2048].rearrange("p (h b i) -> p h b i", h=HEADS, b=2)
        kbd = sb("kbd", [P, PAIRS, 2, WIN + SEQ])
        BD = sb("BD", [P, TILES, HEADS, P])
        BB = sb("BB", [P, HEADS, WIN])
        xst = sb("xst", [P, TILES, DIM])
        xsT = sb("xsT", [P, SEQ + 1])
        x2s = sb("x2s", [P, TILES, DIM])
        x2T = sb("x2T", [P, SEQ + 1])
        xn = sb("xn", [P, TILES, DIM])
        xnT = sb("xnT", [P, SEQ])
        G = sb("G", [P, NF, SEQ])
        H = sb("H", [P, NF, SEQ])
        ss = sb("ss", [P, 5, 2 * HEADS])
        inv = sb("inv", [P, 2 * HEADS])
        mx = sb("mx", [P, HEADS])
        lsum = sb("lsum", [P, 2, HEADS])
        stats = sb("stats", [P, TILES, 6])
        mv = sb("mv", [P, TILES, 2])
        lw = sb("lw", [P, 6, TILES])
        xh = sb("xh", [P, TILES, DIM])
        xhT = sb("xhT", [P, SEQ])
        AqT = sb("AqT", [P, SEQ])
        AkT = sb("AkT", [P, SEQ])
        Vp = sb("Vp", [P, TILES, HA, 32])
        AoT = sb("AoT", [P, 4 * SEQ])
        Arl = sb("Arl", [P, 32])
        AoN = sb("AoN", [P, 4, SEQ])
        Wa = sb("Wa", [P, 3, DIM])
        Wap = sb("Wap", [P, 4, DIM])
        nmx = sb("nmx", [P, 2, 2, HA])

        names = ("d_x d_wa d_c d_qkv d_qks d_wo d_ln d_ff d_out i_const i_zero i_pad i_dve i_pool "
                 "a_lnc a_lnr a_lnn a_xh a_xt a_xe a_qk a_qe a_ke a_km a_v a_ve a_s a_mx a_nm a_e a_t a_te "
                 "a_pv a_oe a_rc a_mu a_on a_wo a_x1 b_lnc b_lnr b_lnn "
                 "s_x s_st s_xt s_xe s_pq s_pk s_pv s_sqq s_sqk s_rq s_rk s_fl s_lg s_iv s_nw s_inv s_qh s_kh "
                 "s_aq s_ak s_bq s_bk s_rot s_tr s_te s_qe s_ke s_sc s_mx s_sub s_exp s_sum s_rl s_pn s_T s_bdc s_bdp "
                 "s_o s_oe s_ve s_wo s_r1 s_x2 s_x2e s_bk2 s_lnc s_lnr s_lnn s_ln s_xn s_xne s_h s_gl s_g s_y s_xc "
                 "s_tab s_fin s_exa")
        S = {n: sem(n) for n in names.split()}
        (d_x, d_wa, d_c, d_qkv, d_qks, d_wo, d_ln, d_ff, d_out, i_const, i_zero, i_pad, i_dve, i_pool,
         a_lnc, a_lnr, a_lnn, a_xh, a_xt, a_xe, a_qk, a_qe, a_ke, a_km, a_v, a_ve, a_s, a_mx, a_nm, a_e, a_t, a_te,
         a_pv, a_oe, a_rc, a_mu, a_on, a_wo, a_x1, b_lnc, b_lnr, b_lnn,
         s_x, s_st, s_xt, s_xe, s_pq, s_pk, s_pv, s_sqq, s_sqk, s_rq, s_rk, s_fl, s_lg, s_iv, s_nw, s_inv, s_qh, s_kh,
         s_aq, s_ak, s_bq, s_bk, s_rot, s_tr, s_te, s_qe, s_ke, s_sc, s_mx, s_sub, s_exp, s_sum, s_rl, s_pn, s_T,
         s_bdc, s_bdp, s_o, s_oe, s_ve, s_wo, s_r1, s_x2, s_x2e, s_bk2, s_lnc, s_lnr, s_lnn, s_ln, s_xn, s_xne,
         s_h, s_gl, s_g, s_y, s_xc, s_tab, s_fin, s_exa) = [S[n] for n in names.split()]

        PJ = [ps[:, 0:2, :].rearrange("p a b -> p (a b)"), ps[:, 2:4, :].rearrange("p a b -> p (a b)")]
        SC = ps[:, 4:6, :]
        TR = [ps[:, 6, :], ps[:, 7, :]]

        N_CONST = 5
        N_WA = 7
        N_FF = 8
        block = ctx.enter_context(nc.Block())

        def attention_steps(eng, a_step):
            a_step(0, True, False, False)
            a_step(1, True, True, False)
            with eng.Fori(2, SEQS) as n:
                a_step(eng.snap(n), True, True, True)
            a_step(SEQS, False, True, True)
            a_step(SEQS + 1, False, False, True)

        def block_slot(i):
            return TR[i % 2] if i < 3 else TR[(i + 1) % 2]

        def block_home(i):
            h = slice(i // 3 * 4, i // 3 * 4 + 4)
            return (PT0[:, h, 0:P], PT0[:, h, P:SEQ], PT1[:, h, :])[i % 3]

        def stack_steps(eng, step):
            step(0, 0, True, False, False, 0)
            step(1, 1, True, True, False, 0)

            def layer_body(base, layer):
                with eng.Fori(0, SEQS - 2) as u:
                    n = eng.snap(base + u + 2)
                    step(n, u + 2, True, True, True, layer)
            with eng.Fori(0, DEPTH - 1) as L:
                layer_body(L * SEQS, L)
                step(eng.snap(L * SEQS + SEQS), 0, True, True, True, L)
                step(eng.snap(L * SEQS + SEQS + 1), 1, True, True, True, L)
            layer_body((DEPTH - 1) * SEQS, DEPTH - 1)
            step(DEPTH * SEQS, 0, False, True, True, DEPTH - 1)
            step(DEPTH * SEQS + 1, 1, False, False, True, DEPTH - 1)

        def unit(u, back):
            if isinstance(u, int):
                k = (u - back) % SEQS * TILES
                return slice(k, k + TILES)
            return bass.ds((u - back) * TILES, TILES)

        @block.sync
        def _(sp):
            sp.dma_start(xres[:, :, :], x_in.rearrange("b (t p) e -> p (b t) e", p=P)).then_inc(d_x, 16)
            for i, w in enumerate((wq_t, wk_t, wv_t)):
                sp.dma_start(Wa[:, i, :], w).then_inc(d_wa, 16)
            for src, dst in ((c_ident, ident[:, :]), (c_causal, causal_f[:, :]),
                             (c_winmask, wmask_f[:, :, :]), (c_headmask, headmask[:, :]),
                             (c_rot, rot[:, :, :, :])):
                sp.dma_start(dst, src).then_inc(d_c, 16)
            sp.wait_ge(i_pad, 2)
            wo_rows = wo_t.rearrange("(c g d) n -> g d c n", g=4, d=DA)
            for g in range(4):
                sp.dma_start(Wap[32 * g:32 * g + DA, :, :], wo_rows[g]).then_inc(d_wa, 16)

            def load_qkv(l):
                sp.dma_start(Wqkv[:, :], wqkv[l]).then_inc(d_qkv, 16)

            def load_scales(l):
                sp.dma_start(qks[:, 0, :], q_scale[l].partition_broadcast(P)).then_inc(d_qks, 16)
                sp.dma_start(qks[:, 1, :], k_scale[l].partition_broadcast(P)).then_inc(d_qks, 16)

            def load_wo(l):
                sp.dma_start(Wo[:, :, :], wo2[l].rearrange("(c p) n -> p c n", p=P)).then_inc(d_wo, 16)

            def load_ln(l):
                sp.dma_start(lng[:, :], ln_g[l].unsqueeze(1)).then_inc(d_ln, 16)
                sp.dma_start(lnb[:, :], ln_b[l].unsqueeze(1)).then_inc(d_ln, 16)

            def load_ff(l):
                sp.dma_start(W1[:, :], w1[l]).then_inc(d_ff, 16)
                last = FCH[-1]
                sp.dma_start(W2[:, 0:NF - 1, :], w2[l][0:last[0], :].rearrange("(c p) n -> p c n", p=P)).then_inc(d_ff, 16)
                sp.dma_start(W2[0:last[1], NF - 1, :], w2[l][last[0]:FF, :]).then_inc(d_ff, 16)
                sp.dma_start(W2[last[1]:last[1] + 1, NF - 1, :], b2[l].unsqueeze(0)).then_inc(d_ff, 16)
                for half in range(2):
                    sp.dma_start(b1s[:, half, 0:NF - 1],
                                 b1[l][half * FF:half * FF + last[0]].rearrange("(c p) -> p c", p=P),
                                 allow_slow_non_contiguous=True).then_inc(d_ff, 16)
                    sp.dma_start(b1s[0:last[1], half, NF - 1:NF],
                                 b1[l][half * FF + last[0]:(half + 1) * FF].unsqueeze(1)).then_inc(d_ff, 16)

            load_scales(0)
            load_qkv(0)
            load_wo(0)
            load_ln(0)
            load_ff(0)
            with sp.Fori(0, DEPTH - 1) as L:
                sp.wait_ge(s_tab, 6 * L + 6)
                load_scales(L + 1)
                sp.wait_ge(s_pv, (L + 1) * SEQS * TILES)
                load_qkv(L + 1)
                sp.wait_ge(s_wo, (L + 1) * SEQS)
                load_wo(L + 1)
                sp.wait_ge(s_xne, (L + 1) * SEQS)
                load_ln(L + 1)
                sp.wait_ge(s_y, (L + 1) * SEQS)
                load_ff(L + 1)
            for q in range(4):
                sp.wait_ge(s_fin, q + 1)
                b = slice(q * SEQS // 4, (q + 1) * SEQS // 4)
                t = slice(q * SEQS * TILES // 4, (q + 1) * SEQS * TILES // 4)
                sp.dma_start(out[b].rearrange("b (t p) e -> p (b t) e", p=P), x1[:, t, :]).then_inc(d_out, 16)
            sp.wait_ge(d_out, 64)

        @block.gpsimd
        def _(pool):
            pool.memset(Vp[:, :, :, :], 0.0).then_inc(i_zero, 1)
            pool.wait_ge(i_zero, 1)
            pool.memset(Vp[:, :, :, DA:DA + 1], 1.0).then_inc(i_zero, 1)
            pool.memset(Wap[:, :, :], 0.0).then_inc(i_pad, 1)
            pool.memset(H[:, :, :], 1.0).then_inc(i_pad, 1)
            pool.memset(kbd[:, :, :, :], 0.0).then_inc(i_zero, 1)
            pool.memset(BD[:, :, :, :], 0.0).then_inc(i_zero, 1)
            pool.memset(xsT[:, :], 0.0).then_inc(i_zero, 1)
            pool.memset(x2T[:, :], 0.0).then_inc(i_zero, 1)
            pool.wait_ge(d_c, 16 * N_CONST)

            def spread_k(n):
                need(pool, a_ke, n + 1)
                need(pool, a_s, 4 * n)
                pool.tensor_tensor(KM[:, :, :], AkT[:, :].unsqueeze(1).broadcast_to([P, HA, SEQ]),
                                   headmask[:, :].unsqueeze(2).broadcast_to([P, HA, SEQ]), ALU.mult).then_inc(a_km, 1)

            spread_k(0)
            with pool.Fori(1, SEQS) as n:
                spread_k(pool.snap(n))
            pool.wait_ge(s_x, SEQS)

            def make_tables(l):
                pool.wait_ge(d_qks, 32 * l + 32)
                need(pool, s_ak, l * (SEQS * TILES))
                h = DH // 2
                for j in range(2):
                    sc = qks[:, j, :].unsqueeze(1).broadcast_to([P, TILES, DH])
                    pool.tensor_tensor(tab[:, :, 2 * j, :], rot[:, :, 2 * j, :], sc, ALU.mult).then_inc(s_tab, 1)
                    pool.tensor_tensor(tab[:, :, 2 * j + 1, 0:h], rot[:, :, 2 * j + 1, 0:h], sc[:, :, h:DH],
                                       ALU.mult).then_inc(s_tab, 1)
                    pool.tensor_tensor(tab[:, :, 2 * j + 1, h:DH], rot[:, :, 2 * j + 1, h:DH], sc[:, :, 0:h],
                                       ALU.mult).then_inc(s_tab, 1)
                pool.wait_ge(s_tab, 6 * l + 6)

            def stage_x(n, u):
                need(pool, s_xt, n)
                need_apart(pool, i_pool, s_x, n + 1)
                pool.tensor_copy(xst[:, :, :], xres[:, unit(u, 0), :]).then_inc(s_st, 1)

            def keep_x2(n, u):
                need_apart(pool, i_pool, s_r1, n)
                pool.tensor_copy(xres[:, unit(u, 1), :], x2s[:, :, :]).then_inc(s_xc, 1)

            def sines(n, t, j):
                T = 2 * n + t
                col = slice(j * INNER, (j + 1) * INNER)
                h = DH // 2
                q4 = QH[:, col].rearrange("p (h d) -> p h d", d=DH)
                b4 = BQ[:, col].rearrange("p (h d) -> p h d", d=DH)
                s4 = tab[:, t, 2 * j + 1, :].unsqueeze(1).broadcast_to([P, HEADS, DH])
                need(pool, (s_qh, s_kh)[j], T + 1)
                need(pool, s_rot, 2 * T - 1 + j)
                pool.tensor_tensor(b4[:, :, 0:h], q4[:, :, h:DH], s4[:, :, 0:h], ALU.mult).then_inc((s_bq, s_bk)[j], 1)
                pool.tensor_tensor(b4[:, :, h:DH], q4[:, :, 0:h], s4[:, :, h:DH], ALU.mult).then_inc((s_bq, s_bk)[j], 1)

            def rotated(n, t, j):
                T = 2 * n + t
                col = slice(j * INNER, (j + 1) * INNER)
                need(pool, (s_bq, s_bk)[j], 2 * T + 2)
                need(pool, (s_aq, s_ak)[j], T + 1)
                pool.tensor_tensor(AQ[t][:, col], AQ[t][:, col], BQ[:, col], ALU.add).then_inc(s_rot, 1)

            def normalise(n, t):
                T = 2 * n + t
                need(pool, s_rl, T + 1)
                p3 = Pr[:, t, :].rearrange("p (h k) -> p h k", h=HEADS)
                pool.tensor_tensor(p3, p3, lsum[:, 1, :].unsqueeze(2).broadcast_to([P, HEADS, 2 * WIN]),
                                   ALU.mult).then_inc(s_pn, 1)

            def step(n, u, head, mid, ffn, layer):
                if head:
                    if isinstance(u, int) and u == 0:
                        make_tables(0 if isinstance(n, int) else layer + 1)
                    stage_x(n, u)
                if mid:
                    normalise(n - 1, 1)
                if head:
                    sines(n, 0, 0)
                    sines(n, 0, 1)
                    rotated(n, 0, 0)
                    rotated(n, 0, 1)
                    sines(n, 1, 0)
                    rotated(n, 1, 0)
                    sines(n, 1, 1)
                    rotated(n, 1, 1)
                if mid:
                    keep_x2(n, u)
                if head:
                    normalise(n, 0)

            stack_steps(pool, step)

        @block.scalar
        def _(act):
            act.preload_act_table_set(TABLE_SET)

            def rsqrt_guess(n, ready, lsem, done):
                need(act, ready, 3 * n + 3)
                act.activation(lw[:, 1, :], lw[:, 0, :], ACT.Ln).then_inc(lsem, 1)
                need(act, lsem, 2 * n + 1)
                act.activation(lw[:, 2, :], lw[:, 1, :], ACT.Exp, scale=-0.5).then_inc(lsem, 1)

            def a_x_evac(n):
                need(act, a_xt, n + 1)
                need(act, a_v, n)
                act.activation(xhT[:, :], TR[0][:, 0:SEQ], ACT.Copy).then_inc(a_xe, 1)

            def a_qk_evac(n):
                need(act, a_qk, n + 1)
                need(act, a_s, 4 * n)
                act.activation(AqT[:, :], TR[1][:, 0:SEQ], ACT.Copy).then_inc(a_qe, 1)
                need(act, a_km, n)
                act.activation(AkT[:, :], TR[1][:, SEQ:2 * SEQ], ACT.Copy).then_inc(a_ke, 1)

            def a_values(n):
                need(act, a_v, n + 1)
                need(act, a_pv, n)
                act.activation(Vp[:, :, :, 0:DA],
                               TR[0][:, 0:SEQ].rearrange("p (t h d) -> p t h d", t=TILES, d=DA), ACT.Copy).then_inc(a_ve, 1)

            def a_exp(n, g):
                if g == 0:
                    need(act, a_t, 12 * n)
                need(act, a_nm, 4 * n + g + 1)
                bank = 3 * (g % 2)
                for h in range(4 * g, 4 * g + 4):
                    k = h - 4 * g
                    act.activation(E0[:, h, :], ps[:, bank, k * P:(k + 1) * P], ACT.Exp,
                                   bias=nmx[:, 1, 0, h:h + 1], scale=A_SCALE)
                    last = act.activation(E1[:, h, :], ps[:, bank + 1 + k // 2, (k % 2) * SEQ:(k % 2 + 1) * SEQ], ACT.Exp,
                                          bias=nmx[:, 1, 1, h:h + 1], scale=A_SCALE)
                last.then_inc(a_e, 1)

            def a_evac(n, g):
                if g == 0:
                    need(act, a_pv, n)
                for j in range(3):
                    i = 3 * g + j
                    need(act, a_t, 12 * n + i + 1)
                    act.activation(block_home(i), block_slot(i).rearrange("p (h q) -> p h q", h=4), ACT.Copy).then_inc(a_te, 1)

            def a_step(n, head, mid, tail):
                if mid:
                    a_exp(n - 1, 0)
                if tail:
                    rsqrt_guess(n - 2, b_lnc, b_lnr, b_lnr)
                if mid:
                    a_evac(n - 1, 0)
                if head:
                    rsqrt_guess(n, a_lnc, a_lnr, a_lnr)
                if mid:
                    a_exp(n - 1, 1)
                if head:
                    a_x_evac(n)
                if mid:
                    a_exp(n - 1, 2)
                if head:
                    a_qk_evac(n)
                if mid:
                    a_evac(n - 1, 1)
                    a_exp(n - 1, 3)
                if head:
                    a_values(n)

            act.wait_ge(i_zero, 2)
            attention_steps(act, a_step)
            act.wait_ge(s_x, SEQS)
            act.wait_ge(i_zero, 6)

            def evac_shifted(dst, sem, n, tr):
                h = DIM // 2
                act.activation(dst[0:h, 0:SEQ], tr[0:h, 0:SEQ], ACT.Copy)
                act.activation(dst[h:DIM, 1:SEQ + 1], tr[h:DIM, 0:SEQ], ACT.Copy).then_inc(sem, 1)

            def x_evac(n):
                need(act, s_xt, n + 1)
                need(act, s_pv, 2 * n)
                evac_shifted(xsT, s_xe, n, TR[1])

            def exps(n, t):
                T = 2 * n + t
                need(act, s_sub, T + 1)
                act.activation(Pr[:, t, :], Pr[:, t, :], ACT.Exp).then_inc(s_exp, 1)

            def gelus(n, chunks):
                for c in chunks:
                    m = FCH[c][1]
                    need(act, s_h, 3 * n + c + 1)
                    act.activation(G[0:m, c, :], TR[c % 2][0:m, SEQ:2 * SEQ], ACT.Gelu,
                                   bias=b1s[0:m, 1, c:c + 1]).then_inc(s_gl, 1)

            def squares(n, t):
                T = 2 * n + t
                need(act, s_pq, T + 1)
                need(act, s_rq, T)
                act.activation(SQ[:, 0:INNER], PJ[t * 0][:, :], ACT.Square).then_inc(s_sqq, 1)
                need(act, s_pk, T + 1)
                need(act, s_rk, T)
                act.activation(SQ[:, INNER:2 * INNER], PJ[1][:, :], ACT.Square).then_inc(s_sqk, 1)

            def norm_guess(n, t):
                T = 2 * n + t
                need(act, s_fl, T + 1)
                act.activation(ss[:, 2, :], ss[:, 1, :], ACT.Ln).then_inc(s_lg, 1)
                need(act, s_lg, T + 1)
                act.activation(ss[:, 3, :], ss[:, 2, :], ACT.Exp, scale=-0.5).then_inc(s_iv, 1)

            def v_evac(n, t):
                T = 2 * n + t
                need(act, s_pv, T + 1)
                need(act, s_o, 2 * 2 * n)
                act.activation(V[:, t, :], PJ[t][:, :], ACT.Copy).then_inc(s_ve, 1)

            def qk_evac(n, t, groups):
                T = 2 * n + t
                for g in groups:
                    tr = TR[g % 2][:, :].rearrange("p (c n) -> p c n", c=4)
                    need(act, s_tr, 4 * T + g + 1)
                    need(act, s_sc, T)
                    c = slice(4 * (g % 2), 4 * (g % 2) + 4)
                    if g < 2:
                        act.activation(qT[:, c, :], tr, ACT.Copy).then_inc(s_te, 1)
                    else:
                        at = slice(WIN + P * t, WIN + P * t + P)
                        act.activation(kbd[0:DH, c, 0, at], tr[0:DH], ACT.Copy)
                        act.activation(kbd[DH:P, c, 1, at], tr[DH:P], ACT.Copy).then_inc(s_te, 1)

            def band_prev(n, t):
                T = 2 * n + t
                need(act, s_T, T + 1)
                need(act, s_o, 2 * T - 2)
                for w in range(NWIN):
                    src = PTr[32 * w:32 * w + 32, :, 0, :]
                    if w:
                        last = act.activation(BD[32 * w - 32:32 * w, t, :, 32 * w:32 * w + 32], src, ACT.Copy)
                    elif t:
                        act.activation(BB[P - WIN:P, :, :], src, ACT.Copy)
                last.then_inc(s_bdp, 1)

            def o_evac_b(n):
                for g in range(2):
                    need(act, s_o, 4 * n + g + 3)
                    need(act, s_oe, 4 * n + 2)
                    act.activation(oT[:, 1, 4 * g:4 * g + 4, :], (TR[0], SC[:, 0, :])[g].rearrange("p (c n) -> p c n", c=4),
                                   ACT.Copy).then_inc(s_oe, 1)

            def x2_evac(n):
                need(act, s_x2, n + 1)
                need(act, s_bk2, n)
                evac_shifted(x2T, s_x2e, n, TR[0])

            def xn_evac(n, layer_wait):
                need(act, s_xn, n + 1)
                need(act, s_h, 3 * n)
                act.wait_ge(d_ln, layer_wait)
                act.activation(xnT[:, :], TR[0][:, 0:SEQ], ACT.Identity, bias=lnb[:, :], scale=lng[:, :]).then_inc(s_xne, 1)

            def step(n, u, head, mid, ffn, layer):
                first = isinstance(u, int) and not isinstance(n, int)
                if head:
                    x_evac(n)
                if mid:
                    exps(n - 1, 1)
                if ffn:
                    act.wait_ge(d_ff, 16 * N_FF * (layer + 1))
                    gelus(n - 2, range(NF - 1))
                if head:
                    squares(n, 0)
                if ffn:
                    gelus(n - 2, (NF - 1,))
                    act.preload_act_table_set(TABLE_SET)
                if head:
                    norm_guess(n, 0)
                if mid:
                    band_prev(n - 1, 1)
                if head:
                    squares(n, 1)
                if mid:
                    o_evac_b(n - 1)
                if head:
                    norm_guess(n, 1)
                    qk_evac(n, 0, range(4))
                if mid:
                    x2_evac(n - 1)
                if head:
                    exps(n, 0)
                if mid:
                    rsqrt_guess(n - 1, s_lnc, s_lnr, s_lnr)
                if head:
                    v_evac(n, 0)
                    qk_evac(n, 1, (0,))
                    v_evac(n, 1)
                    qk_evac(n, 1, (1, 2, 3))
                if mid:
                    later = layer + 1 if first and u == 1 else layer
                    xn_evac(n - 1, 32 * (later + 1))
                if head:
                    band_prev(n, 0)

            stack_steps(act, step)

        @block.vector
        def _(dve):
            def moments(n, chain, src):
                for t in range(TILES):
                    last = dve.bn_stats(stats[:, t, :], src[:, t, :])
                last.then_inc(chain, 1)
                need_apart(dve, i_dve, chain, 3 * n + 1)
                for t in range(TILES):
                    last = dve.bn_aggr(mv[:, t, :], stats[:, t, :])
                last.then_inc(chain, 1)
                dve.wait_ge(chain, 3 * n + 2)
                dve.tensor_scalar(lw[:, 0, :], mv[:, :, 1], EPS, None, ALU.add).then_inc(chain, 1)

            def newton(n, k, v, y0, t1, y1, chain):
                dve.tensor_tensor(t1, y0, y0, ALU.mult).then_inc(chain, 1)
                dve.wait_ge(chain, 4 * n + 1)
                dve.tensor_tensor(t1, t1, v, ALU.mult).then_inc(chain, 1)
                dve.wait_ge(chain, 4 * n + 2)
                dve.tensor_scalar(t1, t1, -0.5, 1.5, ALU.mult, ALU.add).then_inc(chain, 1)
                dve.wait_ge(chain, 4 * n + 3)
                dve.tensor_tensor(y1, y0, t1, ALU.mult).then_inc(chain, 1)
                dve.wait_ge(chain, 4 * n + 4)

            def normalised(n, dst, src, rsem, nsem, done):
                need(dve, rsem, 2 * n + 2)
                newton(n, TILES, lw[:, 0, :], lw[:, 2, :], lw[:, 3, :], lw[:, 4, :], nsem)
                for t in range(TILES):
                    last = dve.tensor_scalar(dst[:, t, :], src[:, t, :], mv[:, t, 0:1], lw[:, 4, t:t + 1],
                                             ALU.subtract, ALU.mult)
                last.then_inc(done, 1)

            dve.wait_ge(d_c, 16 * N_CONST)
            dve.tensor_copy(ident_h[:, :], ident[:, :]).then_inc(i_const, 1)
            dve.tensor_copy(causal[:, :], causal_f[:, :]).then_inc(i_const, 1)
            dve.tensor_copy(wmask[:, :, :], wmask_f[:, :, :]).then_inc(i_const, 1)
            dve.wait_ge(d_x, 16)

            def tiles_of(n):
                return slice(n * TILES, n * TILES + TILES) if isinstance(n, int) else bass.ds(n * TILES, TILES)

            def a_norm(n):
                need(dve, a_xt, n)
                normalised(n, xh, xres[:, tiles_of(n), :], a_lnr, a_lnn, a_xh)

            def a_max(n, g):
                bank = 3 * (g % 2)
                need(dve, a_s, 4 * n + g + 1)
                if g == 0:
                    need(dve, a_e, 4 * n)
                hs = slice(4 * g, 4 * g + 4)
                dve.tensor_reduce(nmx[:, 0, 0, hs], ps[:, bank, :].rearrange("p (h k) -> p h k", h=4), AX.X, ALU.max)
                dve.tensor_reduce(nmx[:, 0, 1, hs], ps[:, bank + 1:bank + 3, :].rearrange("p a (h k) -> p (a h) k", h=2),
                                  AX.X, ALU.max).then_inc(a_mx, 1)
                need(dve, a_mx, 4 * n + g + 1)
                dve.tensor_scalar(nmx[:, 1, :, hs], nmx[:, 0, :, hs], -A_SCALE, None, ALU.mult).then_inc(a_nm, 1)

            def a_evac(n, g):
                if g == 2:
                    need(dve, a_te, 12 * n + 6)
                for j in range(3):
                    i = 3 * g + j
                    need(dve, a_t, 12 * n + i + 1)
                    dve.tensor_copy(block_home(i), block_slot(i).rearrange("p (h q) -> p h q", h=4)).then_inc(a_te, 1)

            def a_divide(n):
                need(dve, a_pv, n + 1)
                dve.transpose(AoT[:, :], ps[:, 3:5, :].rearrange("p a q -> p (a q)")).then_inc(a_oe, 1)
                need(dve, a_oe, n + 1)
                o3 = AoT[:, :].rearrange("p (b r) -> p b r", r=32)
                dve.reciprocal(Arl[:, :], o3[:, :, DA]).then_inc(a_rc, 1)
                need(dve, a_rc, n + 1)
                dve.tensor_tensor(o3, o3, Arl[:, :].unsqueeze(2).broadcast_to([P, 32, 32]), ALU.mult).then_inc(a_mu, 1)
                need(dve, a_mu, n + 1)
                need(dve, a_wo, n)
                dve.transpose(AoN[:, :, :].rearrange("p c q -> p (c q)"), AoT[:, :]).then_inc(a_on, 1)

            def a_residual(n):
                un = tiles_of(n)
                need(dve, a_wo, n + 1)
                dve.tensor_tensor(x1[:, un, :], ps[:, 5, 0:SEQ].rearrange("p (t e) -> p t e", t=TILES), xres[:, un, :],
                                  ALU.add).then_inc(a_x1, 1)
                need_apart(dve, i_dve, a_x1, n + 1)
                moments(n, b_lnc, x1[:, un, :])

            def x1_norm(n):
                normalised(n, xres[:, tiles_of(n), :], x1[:, tiles_of(n), :], b_lnr, b_lnn, s_x)

            def a_step(n, head, mid, tail):
                if mid:
                    a_max(n - 1, 0)
                if tail:
                    a_residual(n - 2)
                if tail:
                    x1_norm(n - 2)
                if head:
                    moments(n, a_lnc, xres[:, tiles_of(n), :])
                if mid:
                    a_max(n - 1, 1)
                if head:
                    a_norm(n)
                if mid:
                    a_max(n - 1, 2)
                    a_max(n - 1, 3)
                    a_evac(n - 1, 2)
                    a_evac(n - 1, 3)
                    a_divide(n - 1)

            attention_steps(dve, a_step)

            def soft_max(n, t):
                T = 2 * n + t
                s3 = SC.rearrange("p a (h k) -> p (a h) k", k=2 * WIN)
                need(dve, s_sc, T + 1)
                dve.tensor_reduce(mx[:, :], s3, AX.X, ALU.max).then_inc(s_mx, 1)
                need(dve, s_mx, T + 1)
                dve.tensor_tensor(Pr[:, t, :].rearrange("p (h k) -> p h k", h=HEADS), s3,
                                  mx[:, :].unsqueeze(2).broadcast_to([P, HEADS, 2 * WIN]), ALU.subtract).then_inc(s_sub, 1)

            def soft_sum(n, t):
                T = 2 * n + t
                need(dve, s_exp, T + 1)
                dve.tensor_reduce(lsum[:, 0, :], Pr[:, t, :].rearrange("p (h k) -> p h k", h=HEADS), AX.X, ALU.add).then_inc(s_sum, 1)
                need(dve, s_sum, T + 1)
                need(dve, s_pn, T)
                dve.reciprocal(lsum[:, 1, :], lsum[:, 0, :]).then_inc(s_rl, 1)

            def turn(n, t):
                T = 2 * n + t
                need(dve, s_pn, T + 1)
                need(dve, s_bdp, T)
                dve.transpose(PTr[:, :, :, :].rearrange("p h b i -> p (h b i)"), Pr[:, t, :]).then_inc(s_T, 1)
                need(dve, s_T, T + 1)
                need(dve, s_o, 2 * T - 2)
                for w in range(NWIN):
                    rows = slice(32 * w, 32 * w + 32)
                    last = dve.tensor_copy(BD[rows, t, :, rows], PTr[rows, :, 1, :])
                last.then_inc(s_bdc, 1)

            def gated(n, chunks):
                for c in chunks:
                    m = FCH[c][1]
                    need(dve, s_gl, 3 * n + c + 1)
                    dve.scalar_tensor_tensor(H[0:m, c, :], TR[c % 2][0:m, 0:SEQ], b1s[0:m, 0, c:c + 1],
                                             G[0:m, c, :], ALU.add, ALU.mult).then_inc(s_g, 1)

            def sum_q(n, t):
                T = 2 * n + t
                need(dve, s_sqq, T + 1)
                dve.tensor_reduce(ss[:, 0, 0:HEADS], SQ[:, 0:INNER].rearrange("p (h d) -> p h d", d=DH), AX.X, ALU.add).then_inc(s_rq, 1)

            def sum_k(n, t):
                T = 2 * n + t
                need(dve, s_sqk, T + 1)
                dve.tensor_reduce(ss[:, 0, HEADS:], SQ[:, INNER:].rearrange("p (h d) -> p h d", d=DH), AX.X, ALU.add).then_inc(s_rk, 1)
                need(dve, s_rk, T + 1)
                dve.tensor_scalar(ss[:, 1, :], ss[:, 0, :], NORM_FLOOR * NORM_FLOOR, None, ALU.max).then_inc(s_fl, 1)

            def over_norms(n, t):
                T = 2 * n + t
                need(dve, s_iv, T + 1)
                newton(T, 2 * HEADS, ss[:, 1, :], ss[:, 3, :], ss[:, 4, :], inv[:, :], s_nw)
                for j in range(2):
                    col = slice(j * INNER, (j + 1) * INNER)
                    need(dve, (s_bq, s_bk)[j], 2 * T)
                    dve.tensor_tensor(QH[:, col].rearrange("p (h d) -> p h d", d=DH),
                                      PJ[j][:, :].rearrange("p (h d) -> p h d", d=DH),
                                      inv[:, j * HEADS:(j + 1) * HEADS].unsqueeze(2).broadcast_to([P, HEADS, DH]),
                                      ALU.mult).then_inc((s_qh, s_kh)[j], 1)
            def cosines(n, t):
                T = 2 * n + t
                for j in range(2):
                    col = slice(j * INNER, (j + 1) * INNER)
                    need(dve, (s_qh, s_kh)[j], T + 1)
                    need(dve, s_tr, 4 * T - 6 + 2 * j)
                    dve.tensor_tensor(AQ[t][:, col].rearrange("p (h d) -> p h d", d=DH),
                                      QH[:, col].rearrange("p (h d) -> p h d", d=DH),
                                      tab[:, t, 2 * j, :].unsqueeze(1).broadcast_to([P, HEADS, DH]),
                                      ALU.mult).then_inc((s_aq, s_ak)[j], 1)

            def residual2(n, u):
                need(dve, s_y, n + 1)
                need(dve, s_xc, n + 1)
                xr = xres[:, unit(u, 2), :]
                dve.tensor_tensor(xr, TR[1][:, 0:SEQ].rearrange("p (t e) -> p t e", t=TILES), xr, ALU.add).then_inc(s_x, 1)

            def o_evac_a(n):
                for g in range(2):
                    need(dve, s_o, 4 * n + g + 1)
                    need(dve, s_wo, n)
                    dve.tensor_copy(oT[:, 0, 4 * g:4 * g + 4, :],
                                    SC[:, g, :].rearrange("p (c n) -> p c n", c=4)).then_inc(s_oe, 1)

            def residual1(n, u):
                need(dve, s_wo, n + 1)
                need(dve, s_xc, n)
                dve.tensor_tensor(x2s[:, :, :], SC[:, 1, 0:SEQ].rearrange("p (t e) -> p t e", t=TILES),
                                  xres[:, unit(u, 1), :], ALU.add).then_inc(s_r1, 1)

            def layer_norm(n):
                src = TR[1][:, 0:SEQ].rearrange("p (t e) -> p t e", t=TILES)
                need_apart(dve, i_dve, s_bk2, n + 1)
                moments(n, s_lnc, src)
                need(dve, s_xn, n)
                normalised(n, xn, src, s_lnr, s_lnn, s_ln)

            def step(n, u, head, mid, ffn, layer):
                if mid:
                    soft_max(n - 1, 1)
                    soft_sum(n - 1, 1)
                if ffn:
                    gated(n - 2, range(NF - 1))
                if head:
                    sum_q(n, 0)
                if ffn:
                    gated(n - 2, (NF - 1,))
                if head:
                    sum_k(n, 0)
                    over_norms(n, 0)
                if mid:
                    turn(n - 1, 1)
                    o_evac_a(n - 1)
                if head:
                    if isinstance(u, int) and u == 0:
                        dve.wait_ge(s_tab, 6 if isinstance(n, int) else 6 * layer + 12)
                    cosines(n, 0)
                    sum_q(n, 1)
                    sum_k(n, 1)
                if ffn:
                    residual2(n - 2, u)
                if head:
                    over_norms(n, 1)
                if mid:
                    residual1(n - 1, u)
                if head:
                    cosines(n, 1)
                    soft_max(n, 0)
                if mid:
                    layer_norm(n - 1)
                if head:
                    soft_sum(n, 0)
                    turn(n, 0)

            stack_steps(dve, step)
            dve.wait_ge(s_x, (DEPTH + 1) * SEQS)
            for q in range(4):
                t = slice(q * SEQS * TILES // 4, (q + 1) * SEQS * TILES // 4)
                dve.tensor_tensor(x1[:, t, :], x1[:, t, :], xres[:, t, :], ALU.add).then_inc(s_fin, 1)

        @block.tensor
        def _(pe):
            mm, tp = pe.matmul, pe.transpose

            def a_turn(n):
                need(pe, a_xh, n + 1)
                for t in range(TILES):
                    last = tp(TR[0][:, t * P:(t + 1) * P], xh[:, t, :], ident[:, :])
                last.then_inc(a_xt, 1)

            def a_project(n):
                need(pe, a_xe, n + 1)
                for i in range(2):
                    last = mm(TR[1][:, i * SEQ:(i + 1) * SEQ], Wa[:, i, :], xhT[:, :], start=True, stop=True)
                last.then_inc(a_qk, 1)

            def a_project_v(n):
                for t in range(TILES):
                    last = mm(TR[0][:, t * P:(t + 1) * P], xhT[:, t * P:(t + 1) * P], Wa[:, 2, :], start=True, stop=True)
                last.then_inc(a_v, 1)

            def a_scores(n, g):
                bank = 3 * (g % 2)
                if g == 0:
                    need(pe, a_km, n + 1)
                    need(pe, a_qe, n + 1)
                if g == 1:
                    need(pe, a_oe, n)
                    need(pe, a_x1, n)
                if g >= 2:
                    need(pe, a_e, 4 * n + g - 1)
                mm(ps[:, bank, :], ident_h[:, :], causal[:, P:2 * P].unsqueeze(1).broadcast_to([P, 4, P]),
                   start=True, stop=False, skip_group_check=True)
                for b in range(2):
                    mm(ps[:, bank + 1 + b, :], ident_h[:, :], causal[:, :].unsqueeze(1).broadcast_to([P, 2, SEQ]),
                       start=True, stop=False, skip_group_check=True)
                for k in range(4):
                    h = 4 * g + k
                    mm(ps[:, bank, k * P:(k + 1) * P], AqT[:, 0:P], KM[:, h, 0:P],
                       start=False, stop=True, skip_group_check=True)
                for k in range(4):
                    h = 4 * g + k
                    last = mm(ps[:, bank + 1 + k // 2, (k % 2) * SEQ:(k % 2 + 1) * SEQ], AqT[:, P:SEQ], KM[:, h, :],
                              start=False, stop=True, skip_group_check=True)
                last.then_inc(a_s, 1)

            def a_transposes(n, g, head):
                need(pe, a_e, 4 * n + g + 1)
                for j in range(3):
                    i = 3 * g + j
                    if i < 2:
                        need(pe, a_ve, n + 1)
                    elif i == 3:
                        need(pe, *((a_xe, n + 2) if head else (a_te, 12 * n + 3)))
                    elif i == 4:
                        need(pe, *((a_ke, n + 2) if head else (a_te, 12 * n + 2)))
                    else:
                        need(pe, a_te, 12 * n + i - 1)
                    for k in range(4):
                        h = 4 * g + k
                        src = (E0[:, h, :], E1[:, h, 0:P], E1[:, h, P:SEQ])[j]
                        last = tp(block_slot(i)[:, k * P:(k + 1) * P], src, ident[:, :])
                    last.then_inc(a_t, 1)

            def a_values(n):
                need(pe, a_te, 12 * n + 12)
                for c in range(4):
                    for g in range(4):
                        h = 4 * c + g
                        o = ps[32 * g:32 * g + 32, 3 + c // 2, (c % 2) * SEQ:(c % 2 + 1) * SEQ]
                        mm(o, Vp[:, 0, h, :], PT0[:, h, :], start=(c % 2 == 0), stop=False, skip_group_check=True)
                for c in range(4):
                    for g in range(4):
                        h = 4 * c + g
                        o = ps[32 * g:32 * g + 32, 3 + c // 2, (c % 2) * SEQ + P:(c % 2 + 1) * SEQ]
                        last = mm(o, Vp[:, 1, h, :], PT1[:, h, :], start=False, stop=True, skip_group_check=True)
                last.then_inc(a_pv, 1)

            def a_output(n):
                need(pe, a_on, n + 1)
                for t in range(TILES):
                    for c in range(4):
                        last = mm(ps[:, 5, t * P:(t + 1) * P], AoN[:, c, t * P:(t + 1) * P], Wap[:, c, :],
                                  start=(c == 0), stop=(c == 3))
                last.then_inc(a_wo, 1)

            def a_step(n, head, mid, tail):
                if mid:
                    a_scores(n - 1, 0)
                if tail:
                    a_output(n - 2)
                if mid:
                    a_scores(n - 1, 1)
                    a_transposes(n - 1, 0, head)
                    a_scores(n - 1, 2)
                if head:
                    if mid:
                        need(pe, a_te, 12 * n - 12 + 3)
                    a_turn(n)
                    a_project(n)
                if mid:
                    a_scores(n - 1, 3)
                    for g in range(1, 4):
                        a_transposes(n - 1, g, head)
                    a_values(n - 1)
                if head:
                    if mid:
                        need(pe, a_te, 12 * n)
                    a_project_v(n)

            pe.wait_ge(d_c, 16 * N_CONST)
            pe.wait_ge(i_const, 3)
            pe.wait_ge(d_wa, 16 * N_WA)
            attention_steps(pe, a_step)
            pe.wait_ge(s_x, SEQS)

            def turn_x(n):
                need(pe, s_st, n + 1)
                for t in range(TILES):
                    last = tp(TR[1][:, t * P:(t + 1) * P], xst[:, t, :], ident[:, :])
                last.then_inc(s_xt, 1)

            def hidden(n, chunks, head):
                need(pe, s_xne, n + 1)
                for c in chunks:
                    f0, m = FCH[c]
                    if c == 1 and head:
                        need(pe, s_xe, n + 3)
                    if c == 2:
                        need(pe, s_g, 3 * n + 1)
                    for half in range(2):
                        last = mm(TR[c % 2][0:m, half * SEQ:(half + 1) * SEQ],
                                  W1[:, half * FF + f0:half * FF + f0 + m], xnT[:, :], start=True, stop=True)
                    last.then_inc(s_h, 1)

            def project(n, t):
                T = 2 * n + t
                need(pe, s_xe, n + 1)
                xt = xsT[:, t * P:(t + 1) * P]
                if t == 0:
                    need(pe, s_ve, T - 1)
                else:
                    need(pe, s_qh, T)
                for b in range(2):
                    last = mm(PJ[0][:, b * 512:(b + 1) * 512], xt, Wqkv[:, b * 512:(b + 1) * 512], start=True, stop=True)
                last.then_inc(s_pq, 1)
                if t == 0:
                    need(pe, s_ve, T)
                else:
                    need(pe, s_kh, T)
                for b in range(2):
                    last = mm(PJ[1][:, b * 512:(b + 1) * 512], xt, Wqkv[:, INNER + b * 512:INNER + (b + 1) * 512],
                              start=True, stop=True)
                last.then_inc(s_pk, 1)

            def project_v(n, t):
                need(pe, (s_qh, s_kh)[t], 2 * n + 2)
                xt = xsT[:, t * P:(t + 1) * P]
                for b in range(2):
                    last = mm(PJ[t][:, b * 512:(b + 1) * 512], xt, Wqkv[:, 2 * INNER + b * 512:2 * INNER + (b + 1) * 512],
                              start=True, stop=True)
                last.then_inc(s_pv, 1)

            def values(n, t):
                T = 2 * n + t
                need(pe, s_bdc, T + 1)
                need(pe, s_bdp, T + 1)
                need(pe, s_ve, T + 1)
                for g in range(2):
                    slot = (SC[:, g, :], (TR[0], SC[:, 0, :])[g])[t]
                    if t == 0 and g == 0:
                        need(pe, s_sub, T + 2)
                    if t == 1 and g == 1:
                        need(pe, s_oe, 4 * n + 1)
                    for c in range(4):
                        for k in range(2):
                            h = 2 * (4 * g + c) + k
                            last = mm(slot[DH * k:DH * k + DH, c * P:(c + 1) * P], V[:, t, h * DH:(h + 1) * DH], BD[:, t, h, :],
                               start=(c == 0), stop=False, skip_group_check=True)
                    for c in range(4):
                        for k in range(2):
                            h = 2 * (4 * g + c) + k
                            if t:
                                last = mm(slot[DH * k:DH * k + DH, c * P:c * P + WIN],
                                          V[P - WIN:P, 0, h * DH:(h + 1) * DH], BB[P - WIN:P, h, :],
                                          start=False, stop=True, skip_group_check=True)
                    last.then_inc(s_o, 1)

            def output(n):
                for t in range(TILES):
                    need(pe, s_oe, 4 * n + 2 * t + 2)
                    for c in range(PAIRS):
                        last = mm(SC[:, 1, t * P:(t + 1) * P], oT[:, t, c, :], Wo[:, c, :],
                                  start=(c == 0), stop=(c == PAIRS - 1))
                last.then_inc(s_wo, 1)

            def turn_qk(n, t, ffn=False):
                T = 2 * n + t
                for g in range(4):
                    if g in (0, 2):
                        need(pe, s_rot, 2 * T + g // 2 + 1)
                    if g >= 2:
                        need(pe, s_te, 4 * T + g - 1)
                    elif t == 1:
                        if g == 0:
                            need(pe, s_x2e, n)
                        else:
                            need(pe, s_ln, n)
                    elif g == 1 and ffn:
                        need(pe, s_x, SEQS + n - 1)
                    for c in range(4):
                        q0 = g * 512 + c * P
                        last = tp(TR[g % 2][:, c * P:(c + 1) * P], AQ[t][:, q0:q0 + P], ident[:, :])
                    last.then_inc(s_tr, 1)

            def scores(n, t, mid=False):
                T = 2 * n + t
                need(pe, s_te, 4 * T + 4)
                need(pe, s_sub, T)
                if mid:
                    need(pe, s_r1, n)
                for b in range(2):
                    mm(SC[:, b, :], ident_h[:, :], wmask[:, t, :].unsqueeze(1).broadcast_to([P, 8, 2 * WIN]),
                       start=True, stop=False, skip_group_check=True)
                for c in range(PAIRS):
                    for w in range(NWIN):
                        k0 = P * t + WIN * w
                        last = mm(SC[32 * w:32 * w + 32, c // 4, (c % 4) * P:(c % 4 + 1) * P],
                                  qT[:, c, 32 * w:32 * w + 32], kbd[:, c, :, k0:k0 + 2 * WIN],
                                  start=False, stop=True, skip_group_check=True)
                last.then_inc(s_sc, 1)

            def turn_x2(n):
                need(pe, s_r1, n + 1)
                for t in range(TILES):
                    last = tp(TR[0][:, t * P:(t + 1) * P], x2s[:, t, :], ident[:, :])
                last.then_inc(s_x2, 1)

            def turn_back(n, tail):
                need(pe, s_x2e, n + 1)
                if tail:
                    need(pe, s_x, SEQS + n)
                for t in range(TILES):
                    last = tp(TR[1][:, t * P:(t + 1) * P], x2T[:, t * P:(t + 1) * P], ident[:, :])
                last.then_inc(s_bk2, 1)

            def turn_xn(n, head):
                need(pe, s_ln, n + 1)
                if head:
                    need(pe, s_te, 4 * (2 * n + 3) + 3)
                for t in range(TILES):
                    last = tp(TR[0][:, t * P:(t + 1) * P], xn[:, t, :], ident[:, :])
                last.then_inc(s_xn, 1)

            def feed_out(n):
                need(pe, s_g, 3 * n + 3)
                for t in range(TILES):
                    for c, (_, m) in enumerate(FCH):
                        k = m + (c == NF - 1)
                        last = mm(TR[1][:, t * P:(t + 1) * P], H[0:k, c, t * P:(t + 1) * P], W2[0:k, c, :],
                                  start=(c == 0), stop=(c == NF - 1))
                last.then_inc(s_y, 1)

            def step(n, u, head, mid, ffn, layer):
                if head:
                    turn_x(n)
                if ffn:
                    pe.wait_ge(d_ff, 16 * N_FF * (layer + 1))
                    hidden(n - 2, range(NF - 1), head)
                if head:
                    if isinstance(u, int) and u == 0:
                        pe.wait_ge(d_qkv, 16 if isinstance(n, int) else 16 * (layer + 2))
                    project(n, 0)
                if ffn:
                    hidden(n - 2, (NF - 1,), head)
                if mid:
                    values(n - 1, 0)
                if ffn:
                    feed_out(n - 2)
                if head:
                    project(n, 1)
                if mid:
                    values(n - 1, 1)
                    if isinstance(u, int) and u == 1:
                        pe.wait_ge(d_wo, 16 if isinstance(n, int) else 16 * (layer + 2))
                    output(n - 1)
                if head:
                    turn_qk(n, 0, ffn)
                    scores(n, 0, mid)
                if mid:
                    turn_x2(n - 1)
                if head:
                    project_v(n, 0)
                if mid:
                    turn_back(n - 1, not head)
                if head:
                    project_v(n, 1)
                    turn_qk(n, 1)
                if mid:
                    turn_xn(n - 1, head)
                if head:
                    scores(n, 1)

            stack_steps(pe, step)


def constants():
    import numpy as np
    f = np.float32
    low = f(-3.0e38)
    i = np.arange(P)
    win = np.zeros((P, 2, 2 * WIN), f)
    c = np.arange(2 * WIN)[None, :]
    r = (i % WIN)[:, None]
    hidden = (r < c - WIN) | (r > c)
    win[:, 0] = np.where(hidden | ((i[:, None] < WIN) & (c < WIN)), low, f(0))
    win[:, 1] = np.where(hidden, low, f(0))
    causal = np.zeros((P, 2 * P), f)
    causal[:, P:] = np.where(i[None, :] > i[:, None], low, f(0))
    headmask = (i[:, None] // DA == np.arange(HA)[None, :]).astype(f)
    half = np.arange(0, DH, 2, dtype=f)
    inv_freq = f(1.0) / f(10000.0) ** (half / f(DH))
    t = np.arange(SEQ, dtype=f)
    freqs = (t[:, None] * inv_freq[None, :]).astype(f)
    base = (half + f(0.4 * DH)) / f(1.4 * DH)
    scale = base[None, :] ** ((t - f(SEQ // 2)) / f(WIN // 2))[:, None]
    cos, sin = np.cos(freqs), np.sin(freqs)
    tabs = np.stack([np.concatenate([cos * scale, cos * scale], 1) * f(QK_SCALE),
                     np.concatenate([-sin * scale, sin * scale], 1) * f(QK_SCALE),
                     np.concatenate([cos / scale, cos / scale], 1),
                     np.concatenate([-sin / scale, sin / scale], 1)], 1).astype(f)
    rot = np.ascontiguousarray(tabs.reshape(TILES, P, 4, DH).transpose(1, 0, 2, 3))
    return [np.eye(P, dtype=f), win, causal, headmask, rot]


def kernel(**inputs):
    import numpy as _np
    import concourse.bacc as _bacc
    from concourse.bass_utils import run_bass_kernel_spmd as _run

    nc = _bacc.Bacc("TRN2", target_bir_lowering=False, num_devices=1)
    arrays, args = {}, []

    def give(name, a):
        a = _np.ascontiguousarray(a)
        arrays[name] = a
        args.append(nc.dram_tensor(name, a.shape, mybir.dt.from_np(a.dtype), kind="ExternalInput").ap())

    give("x", inputs["L0_attn_x"])
    for w in ("Wq", "Wk", "Wv", "Wo"):
        give(w + "_t", _np.asarray(inputs["L0_attn_" + w]).T)
    for w in ("Wqkv", "q_scale", "k_scale", "Wo", "ln_g", "ln_b", "W1", "b1", "W2", "b2"):
        give("ffn_" + w, inputs["L0_ffn_" + w])
    for i, a in enumerate(constants()):
        give(f"const_{i}", a)
    args.append(nc.dram_tensor("out_0", (SEQS, SEQ, DIM), F32, kind="ExternalOutput").ap())
    build(nc, *args)
    r = _run(nc, [arrays], core_ids=[0])
    return r.results[0]["out_0"]
```
